# Optimizing a Trainium2 kernel written in Bass

```python
import numpy as np
import jax
import jax.numpy as jnp

def _softmax(x, axis=-1):
    return jax.nn.softmax(x, axis=axis)

def _gelu(x):
    return jax.nn.gelu(x, approximate=True)

def _silu(x):
    return jax.nn.silu(x)

def _sigmoid(x):
    return jax.nn.sigmoid(x)

def _layernorm(x, axis=-1, eps=1e-05):
    m = jnp.mean(x, axis=axis, keepdims=True)
    v = jnp.var(x, axis=axis, keepdims=True)
    return (x - m) / jnp.sqrt(v + eps)

def _scatter_add(tgt, idx, src, axis=0):
    return tgt.at[idx].add(src)

def _segment_sum(src, seg, n):
    return jax.ops.segment_sum(src, seg, n)
kernel_name = 'mk_seq_preln_d1_jaxref_r8_710799'

def setup_inputs(seed: int=0):
    np.random.seed(seed)
    _w = jnp.asarray

    def _L0_attn_setup():
        import jax, jax.numpy as jnp
        import numpy as np
        CHUNK = 32

        def _l2norm(x):
            return x * jax.lax.rsqrt(jnp.sum(x * x, -1, keepdims=True) + 1e-06)

        def _short_conv(x, w):
            K = w.shape[-1]
            L = x.shape[1]
            xp = jnp.pad(x, ((0, 0), (K - 1, 0), (0, 0)))
            y = sum((xp[:, t:t + L, :] * w[:, t] for t in range(K)))
            return jax.nn.silu(y)

        def _fir_conv(x, w):
            B, L, H, D = x.shape
            K = w.shape[-1]
            xf = x.reshape(B, L, H * D).transpose(0, 2, 1)
            wf = w.reshape(H * D, 1, K)
            y = jax.lax.conv_general_dilated(xf, wf, (1,), [(K - 1, 0)], feature_group_count=H * D, dimension_numbers=('NCH', 'OIH', 'NCH'))
            return y.transpose(0, 2, 1).reshape(B, L, H, D)

        def _delta_rule(q, k, v, beta, chunk=CHUNK):
            B, H, L, Dk = q.shape
            Dv = v.shape[-1]
            pad = -L % chunk
            if pad:
                q, k, v = (jnp.pad(t, ((0, 0), (0, 0), (0, pad), (0, 0))) for t in (q, k, v))
                beta = jnp.pad(beta, ((0, 0), (0, 0), (0, pad)))
            Lp = L + pad
            n = Lp // chunk
            q = _l2norm(q)
            k = _l2norm(k)
            v = v * beta[..., None]
            kb = k * beta[..., None]
            resh = lambda t: t.reshape(B, H, n, chunk, -1)
            q, k, v, kb = map(resh, (q, k, v, kb))
            tri = jnp.triu(jnp.ones((chunk, chunk), bool))
            tri_s = jnp.triu(tri, 1)
            A = jnp.where(tri, 0.0, -jnp.einsum('bhncd,bhnmd->bhncm', kb, k))
            for i in range(1, chunk):
                A = A.at[..., i, :i].add(jnp.einsum('...j,...jk->...k', A[..., i, :], A[..., :, :i]))
            T = A + jnp.eye(chunk, dtype=A.dtype)
            u = T @ v
            w = T @ kb

            def step(S, inp):
                qi, ki, ui, wi = inp
                attn = jnp.where(tri_s, 0.0, qi @ jnp.swapaxes(ki, -1, -2))
                u_i = ui - wi @ S
                o = qi @ S + attn @ u_i
                S = S + jnp.swapaxes(ki, -1, -2) @ u_i
                return (S, o)
            S0 = jnp.zeros((B, H, Dk, Dv), q.dtype)
            blocks = lambda t: jnp.moveaxis(t, 2, 0)
            S, out = jax.lax.scan(step, S0, (blocks(q), blocks(k), blocks(u), blocks(w)))
            out = jnp.moveaxis(out, 0, 2).reshape(B, H, Lp, Dv)[:, :, :L]
            return (out, S)
        key = jax.random.key(seed)
        B, L, D, H = (2, 256, 128, 4)
        Dv = D // H
        ks = jax.random.split(key, 16)
        nrm = lambda k, s, sc: jax.random.normal(k, s, jnp.float32) * sc
        gate_in_dim = D + 2 * H * 4
        hid = 2 * D
        return {'hidden_states': nrm(ks[0], (B, L, D), 1.0), 'Wq': nrm(ks[1], (D, D), D ** (-0.5)), 'Wk': nrm(ks[2], (D, D), D ** (-0.5)), 'Wv': nrm(ks[3], (D, D), D ** (-0.5)), 'Wb': nrm(ks[4], (H, D), D ** (-0.5)), 'qconv_w': nrm(ks[5], (D, 4), 0.5), 'kconv_w': nrm(ks[6], (D, 4), 0.5), 'vconv_w': nrm(ks[7], (D, 4), 0.5), 'fir_short_w': jnp.zeros((H, Dv, 3)).at[..., -1].set(1.0) + nrm(ks[8], (H, Dv, 3), 0.02), 'fir_long_w': jnp.zeros((H, Dv, 63)).at[..., -1].set(1.0) + nrm(ks[9], (H, Dv, 63), 0.02), 'gate_w1': nrm(ks[10], (hid, gate_in_dim), gate_in_dim ** (-0.5)), 'gate_b1': jnp.zeros((hid,), jnp.float32), 'gate_w2': nrm(ks[11], (H * 4, hid), hid ** (-0.5)), 'log_temp': jnp.zeros((H,), jnp.float32), 'base_bias': jnp.zeros((H, 4)).at[:, 3].set(2.0), 'floor_raw': jnp.full((H, 4), float(np.log(0.5)), jnp.float32), 'onorm_w': jnp.ones((Dv,), jnp.float32), 'Wo': nrm(ks[12], (D, D), D ** (-0.5))}
    _L0_attn_in = _L0_attn_setup()

    def _L0_ffn_setup():
        import jax, jax.numpy as jnp
        import numpy as np
        B, S, H, I, E, K = (2, 256, 128, 256, 8, 2)
        key = jax.random.key(seed)
        k1, k2, k3, k4, k5 = jax.random.split(key, 5)
        scale_h = 1.0 / np.sqrt(H)
        scale_i = 1.0 / np.sqrt(I)
        return {'x': jax.random.normal(k1, (B, S, H), dtype=jnp.float32), 'Wg': jax.random.normal(k2, (H, E), dtype=jnp.float32) * scale_h, 'W11': jax.random.normal(k3, (E, H, I), dtype=jnp.float32) * scale_h, 'W12': jax.random.normal(k4, (E, H, I), dtype=jnp.float32) * scale_h, 'W2': jax.random.normal(k5, (E, I, H), dtype=jnp.float32) * scale_i}
    _L0_ffn_in = _L0_ffn_setup()
    _d = {'L0_attn_hidden_states': _L0_attn_in['hidden_states'], 'L0_attn_Wq': _L0_attn_in['Wq'], 'L0_attn_Wk': _L0_attn_in['Wk'], 'L0_attn_Wv': _L0_attn_in['Wv'], 'L0_attn_Wb': _L0_attn_in['Wb'], 'L0_attn_qconv_w': _L0_attn_in['qconv_w'], 'L0_attn_kconv_w': _L0_attn_in['kconv_w'], 'L0_attn_vconv_w': _L0_attn_in['vconv_w'], 'L0_attn_fir_short_w': _L0_attn_in['fir_short_w'], 'L0_attn_fir_long_w': _L0_attn_in['fir_long_w'], 'L0_attn_gate_w1': _L0_attn_in['gate_w1'], 'L0_attn_gate_b1': _L0_attn_in['gate_b1'], 'L0_attn_gate_w2': _L0_attn_in['gate_w2'], 'L0_attn_log_temp': _L0_attn_in['log_temp'], 'L0_attn_base_bias': _L0_attn_in['base_bias'], 'L0_attn_floor_raw': _L0_attn_in['floor_raw'], 'L0_attn_onorm_w': _L0_attn_in['onorm_w'], 'L0_attn_Wo': _L0_attn_in['Wo'], 'L0_ffn_Wg': _L0_ffn_in['Wg'], 'L0_ffn_W11': _L0_ffn_in['W11'], 'L0_ffn_W12': _L0_ffn_in['W12'], 'L0_ffn_W2': _L0_ffn_in['W2']}
    _x0 = _d['L0_attn_hidden_states']
    _d['L0_attn_hidden_states'] = jax.random.normal(jax.random.fold_in(jax.random.key(seed), 1), (8, 256, 128), dtype=_x0.dtype)
    del _x0
    return _d

def reference(L0_attn_hidden_states, L0_attn_Wq, L0_attn_Wk, L0_attn_Wv, L0_attn_Wb, L0_attn_qconv_w, L0_attn_kconv_w, L0_attn_vconv_w, L0_attn_fir_short_w, L0_attn_fir_long_w, L0_attn_gate_w1, L0_attn_gate_b1, L0_attn_gate_w2, L0_attn_log_temp, L0_attn_base_bias, L0_attn_floor_raw, L0_attn_onorm_w, L0_attn_Wo, L0_ffn_Wg, L0_ffn_W11, L0_ffn_W12, L0_ffn_W2):

    def _L0_attn_ref(hidden_states, Wq, Wk, Wv, Wb, qconv_w, kconv_w, vconv_w, fir_short_w, fir_long_w, gate_w1, gate_b1, gate_w2, log_temp, base_bias, floor_raw, onorm_w, Wo):
        import jax, jax.numpy as jnp
        import numpy as np
        CHUNK = 32

        def _l2norm(x):
            return x * jax.lax.rsqrt(jnp.sum(x * x, -1, keepdims=True) + 1e-06)

        def _short_conv(x, w):
            K = w.shape[-1]
            L = x.shape[1]
            xp = jnp.pad(x, ((0, 0), (K - 1, 0), (0, 0)))
            y = sum((xp[:, t:t + L, :] * w[:, t] for t in range(K)))
            return jax.nn.silu(y)

        def _fir_conv(x, w):
            B, L, H, D = x.shape
            K = w.shape[-1]
            xf = x.reshape(B, L, H * D).transpose(0, 2, 1)
            wf = w.reshape(H * D, 1, K)
            y = jax.lax.conv_general_dilated(xf, wf, (1,), [(K - 1, 0)], feature_group_count=H * D, dimension_numbers=('NCH', 'OIH', 'NCH'))
            return y.transpose(0, 2, 1).reshape(B, L, H, D)

        def _delta_rule(q, k, v, beta, chunk=CHUNK):
            B, H, L, Dk = q.shape
            Dv = v.shape[-1]
            pad = -L % chunk
            if pad:
                q, k, v = (jnp.pad(t, ((0, 0), (0, 0), (0, pad), (0, 0))) for t in (q, k, v))
                beta = jnp.pad(beta, ((0, 0), (0, 0), (0, pad)))
            Lp = L + pad
            n = Lp // chunk
            q = _l2norm(q)
            k = _l2norm(k)
            v = v * beta[..., None]
            kb = k * beta[..., None]
            resh = lambda t: t.reshape(B, H, n, chunk, -1)
            q, k, v, kb = map(resh, (q, k, v, kb))
            tri = jnp.triu(jnp.ones((chunk, chunk), bool))
            tri_s = jnp.triu(tri, 1)
            A = jnp.where(tri, 0.0, -jnp.einsum('bhncd,bhnmd->bhncm', kb, k))
            for i in range(1, chunk):
                A = A.at[..., i, :i].add(jnp.einsum('...j,...jk->...k', A[..., i, :], A[..., :, :i]))
            T = A + jnp.eye(chunk, dtype=A.dtype)
            u = T @ v
            w = T @ kb

            def step(S, inp):
                qi, ki, ui, wi = inp
                attn = jnp.where(tri_s, 0.0, qi @ jnp.swapaxes(ki, -1, -2))
                u_i = ui - wi @ S
                o = qi @ S + attn @ u_i
                S = S + jnp.swapaxes(ki, -1, -2) @ u_i
                return (S, o)
            S0 = jnp.zeros((B, H, Dk, Dv), q.dtype)
            blocks = lambda t: jnp.moveaxis(t, 2, 0)
            S, out = jax.lax.scan(step, S0, (blocks(q), blocks(k), blocks(u), blocks(w)))
            out = jnp.moveaxis(out, 0, 2).reshape(B, H, Lp, Dv)[:, :, :L]
            return (out, S)
        B, L, D = hidden_states.shape
        H = log_temp.shape[0]
        P = 4
        q = _short_conv(hidden_states @ Wq.T, qconv_w).reshape(B, L, H, -1)
        k = _short_conv(hidden_states @ Wk.T, kconv_w).reshape(B, L, H, -1)
        v = _short_conv(hidden_states @ Wv.T, vconv_w).reshape(B, L, H, -1)
        beta = jax.nn.sigmoid(hidden_states @ Wb.T)
        tr = lambda t: jnp.swapaxes(t, 1, 2)
        delta, _S = _delta_rule(tr(q), tr(k), tr(v), jnp.swapaxes(beta, 1, 2))
        delta = jnp.swapaxes(delta, 1, 2)
        short = _fir_conv(v, fir_short_w)
        longp = _fir_conv(v, fir_long_w)
        paths = (short, longp, delta, v)

        def stats(p):
            m = p.mean(-1)
            va = p.var(-1)
            return jnp.stack([m, va], -1).reshape(B, L, H * 2)
        gate_in = jnp.concatenate([hidden_states] + [stats(p) for p in paths], -1)
        hmid = jax.nn.gelu(gate_in @ gate_w1.T + gate_b1, approximate=False)
        logits = hmid @ gate_w2.T + base_bias.reshape(-1)
        temp = jax.nn.softplus(log_temp) + 0.0001
        logits = logits.reshape(B, L, H, P) / temp[None, None, :, None]
        probs = jax.nn.softmax(logits, -1)
        floor_val = 0.05 * jax.nn.sigmoid(floor_raw)
        probs = jnp.maximum(probs, floor_val)
        probs = probs / probs.sum(-1, keepdims=True)
        out = sum((probs[..., i, None] * p for i, p in enumerate(paths)))
        out = out * jax.lax.rsqrt(jnp.mean(out * out, -1, keepdims=True) + 1e-05) * onorm_w
        return out.reshape(B, L, -1) @ Wo.T

    def _L0_ffn_ref(x, Wg, W11, W12, W2):
        import jax, jax.numpy as jnp
        import numpy as np
        B, S, H, I, E, K = (2, 256, 128, 256, 8, 2)
        gate_scores = jax.nn.softmax(x @ Wg, axis=-1)
        topk_scores, topk_idx = jax.lax.top_k(gate_scores, K)
        topk_scores = topk_scores / (topk_scores.sum(-1, keepdims=True) + 1e-08)
        gate = jnp.einsum('bsh,ehi->bsei', x, W11)
        value = jnp.einsum('bsh,ehi->bsei', x, W12)
        fused = gate * jax.nn.sigmoid(gate) * value
        expert_out = jnp.einsum('bsei,eih->bseh', fused, W2)
        gathered = jnp.take_along_axis(expert_out, topk_idx[..., None], axis=2)
        out = jnp.sum(topk_scores[..., None] * gathered, axis=2)
        return out
    x = L0_attn_hidden_states
    x = x + _L0_attn_ref(_layernorm(x, axis=-1), L0_attn_Wq, L0_attn_Wk, L0_attn_Wv, L0_attn_Wb, L0_attn_qconv_w, L0_attn_kconv_w, L0_attn_vconv_w, L0_attn_fir_short_w, L0_attn_fir_long_w, L0_attn_gate_w1, L0_attn_gate_b1, L0_attn_gate_w2, L0_attn_log_temp, L0_attn_base_bias, L0_attn_floor_raw, L0_attn_onorm_w, L0_attn_Wo)
    x = x + _L0_ffn_ref(_layernorm(x, axis=-1), L0_ffn_Wg, L0_ffn_W11, L0_ffn_W12, L0_ffn_W2)
    return x

_drawn_inputs = setup_inputs


def setup_inputs(seed=0):
    import zlib

    import numpy as np

    out = dict(_drawn_inputs(seed))
    spreads = {'L0_attn_gate_b1': (0.0, 0.513),
     'L0_attn_log_temp': (0.0, 1.69),
     'L0_attn_floor_raw': (-0.6931471824645996, 0.6),
     'L0_attn_onorm_w': (1.0, 0.2)}
    factors = {'L0_attn_fir_short_w': 4.611}
    for name, (base, spread) in spreads.items():
        noise = np.random.default_rng([zlib.crc32(name.encode()), seed]).standard_normal(out[name].shape)
        drawn = base * np.exp(spread * noise) if base else spread * noise
        out[name] = jnp.asarray(drawn.astype(out[name].dtype))
    for name, factor in factors.items():
        out[name] = (out[name] * factor).astype(out[name].dtype)
    return out
```

```python
from contextlib import ExitStack

import concourse.bass as bass
from concourse import mybir

F32 = mybir.dt.float32
ALU = mybir.AluOpType
ACT = mybir.ActivationFunctionType
AX = mybir.AxisListType

P = 128
B, L, D = 8, 256, 128
H, DH = 4, 32
C = 32
NPAIR = B // 2
TOK = 2 * L
NT = TOK // P
M = TOK // C
NC = L // C
HB = C // 2
KS, KL = 3, 63
LAGS = 3
NP = 4
HID = 256
E, FF = 8, 256
FC = FF // P

A_VEC, A_POOL = 28, 28
B_VEC = 16
V_VEC = 8


def build(nc, x, wqT, wkT, wvT, wbT, qcw, kcw, vcw, fsw, flr, w1xT, w1sT, b1, w2T, ltemp, bbias, froor, onw, woT,
          wg, w11, w12, w2, out):
    ctx = ExitStack()
    with ctx:
        def sb(name, *shape):
            return ctx.enter_context(nc.sbuf_tensor(name, [P, *shape], F32))

        def sem(name):
            return ctx.enter_context(nc.semaphore(name))

        x_sb = sb("x_sb", 2 * B, D)
        xnp = sb("xnp", B, KS + L)
        v_hc = sb("v_hc", B, 2 + NC, DH)
        short_hc = sb("short_hc", B * NC, DH)
        long_hc = sb("long_hc", B * NC, DH)
        toep_room = sb("toep_room", DH * LAGS * C)
        toep = toep_room[:, :].rearrange("p (c k) -> p c k", c=DH)
        wq_sb, wk_sb, wv_sb = sb("wq_sb", D), sb("wk_sb", D), sb("wv_sb", D)
        wqc, wkc, wvc = sb("wqc", 4, D), sb("wkc", 4, D), sb("wvc", 4, D)
        taps = sb("taps", 3, 4, D)
        wbe = sb("wbe", H, C)
        wb_sb = sb("wb_sb", H)
        fs_sb = sb("fs_sb", KS)
        w1x, w1s = sb("w1x", HID), sb("w1s", HID)
        b1_sb = sb("b1_sb", 2)
        w2e = sb("w2e", 2, H, C)
        w2r = sb("w2r", 2, H * NP)
        wo_sb = sb("wo_sb", D)
        wg_sb = sb("wg_sb", E)
        w11_sb, w12_sb = sb("w11_sb", E, FF), sb("w12_sb", E, FF)
        w2_sb = sb("w2_sb", E * FC, D)
        temp, bias_hc, floor_hc, on_sb = sb("temp", 4), sb("bias_hc", NP), sb("floor_hc", NP), sb("on_sb", DH)
        ones, ident = sb("ones", P), sb("ident", P)
        neg_low = sb("neg_low", DH)
        keep_up = sb("keep_up", DH)
        off_up = sb("off_up", DH)
        mh = sb("mh", 64)
        id16 = sb("id16", HB, HB)

        cen = sb("cen", NT, D)
        sq = sb("sq", NT, D)
        st = sb("st", 4, 16)
        v_room = sb("v_room", 5 * TOK + 4)
        vf = v_room[:, 4 * TOK:5 * TOK + 4].rearrange("p (b l) -> p b l", b=2)
        vt, sft = (v_room[:, TOK * k:TOK * k + TOK].rearrange("p (m c) -> p m c", c=C) for k in (0, 1))
        sf0, sf1 = (v_room[:, TOK * k:TOK * k + TOK].rearrange("p (b l) -> p b l", b=2) for k in (2, 3))
        qf, kf, tb = sb("qf", M, C), sb("kf", M, C), sb("tb", M, C)
        qk_hc = sb("qk_hc", 2, M, DH)
        qk_sq = sb("qk_sq", 2, M, DH)
        ss, rn = sb("ss", 2, M), sb("rn", 2, M)
        bt, beta = sb("bt", M, C), sb("beta", M, C)
        qn, kn = sb("qn", M, DH), sb("kn", M, DH)
        kq_t = sb("kq_t", 2, M, C)
        kb, vb = sb("kb", M, DH), sb("vb", M, DH)
        nbm = sb("nbm", M, C)
        a_hc, a_t, a_off_t = sb("a_hc", M, C), sb("a_t", M, C), sb("a_off_t", M, C)
        attn_t = sb("attn_t", M, C)
        a_it, t_it, prod = sb("a_it", HB, HB), sb("t_it", HB, HB), sb("prod", HB * HB)
        t16, t16_t, y_sb = sb("t16", M, C), sb("t16_t", M, C), sb("y_sb", M, C)
        t32_t, wneg_t = sb("t32_t", M, C), sb("wneg_t", M, C)
        u_sb, s_sb = sb("u_sb", 2, DH), sb("s_sb", 2, DH)
        paths = sb("paths", NP, M, DH)
        psq = sb("psq", NP, M, DH)
        pcen = toep_room[:, 0:NP * TOK].rearrange("p (a m d) -> p a m d", a=NP, m=M)
        psum_, pvar = sb("psum_", NP, M), sb("pvar", NP, M)
        stats, stats_t = sb("stats", M, C), sb("stats_t", M, C)
        hm = sb("hm", 2, TOK)
        lg = sb("lg", M, C)
        lb = sb("lb", M, NP)
        g0, g1, pr = sb("g0", M), sb("g1", M), sb("pr", M, NP)
        oh = sb("oh", M, DH)
        o_t = sb("o_t", TOK)
        x1 = sb("x1", 1, NT, D)
        cen2, sq2 = cen, sq
        st2 = sb("st2", 4, NT)
        x2t = sb("x2t", TOK)
        rs, rt, ru = sb("rs", NT, E), sb("rt", NT, E), sb("ru", NT, E)
        cmp, cmq = sb("cmp", NT, E, E), sb("cmq", NT, E, E)
        before, after = sb("before", E, E), sb("after", E, E)
        sg = toep_room[:, NP * TOK:(NP + 2) * TOK].rearrange("p (k n) -> p k n", k=2)
        fu = v_room[:, 0:4 * TOK].rearrange("p (k f n) -> p k f n", k=2, f=FC)

        ps = [ctx.enter_context(nc.psum_tensor(f"ps{i}", [P, 512], F32)) for i in range(8)]
        lanes = [ps[i][:, :] for i in range(3)]

        shear_d = nc.dram_tensor("shear_d", [C, D, LAGS * C], F32).ap()
        a_d = nc.dram_tensor("a_d", [M, P, C], F32).ap()
        t_d = nc.dram_tensor("t_d", [M, P, C], F32).ap()

        names = """w_loaded x_loaded consts_ready pool_consts padw_ready pw_stored toep_loaded wb_expanded
        xn_ready xt_done xt_copied v_proj v_silu vt_ready v_copied sft_ready s_copied ln_sq ln_ms ln_rs pads_zero
        t_zeroed fir_done long_ready sm_exp0 vp_vec vp_act
        qkb_done q_silu k_silu b_tanh qk_ready qk_squared ms_ready rn_ready beta_ready kq_ready kbvb_ready nbm_ready g_done
        a_ready attn_ready at_ready aoff_ready a_stored a_items t_items t_stored t16_loaded t16t_ready y_done
        y_ready t32_done t32_ready w_done w_ready u_done s_done o_done
        p_copied delta_ready cen_ready psq_ready stats_ready hmid_done hm_ready lg_done ex_in ex_out mix_ready osq_ready om_ready orn_ready
        ot_ready wo_done x1_ready
        b_cen b_sq b_ms b_rs xn2_ready x2t_done x2t_ready r_done r_in r_ex gate_done val_done sg_ready fu_ready y2_done acc_done
        out_stored a_vec b_vec a_pool a_act""".split()
        s = {n: sem(n) for n in names}
        u_ready = [sem(f"u_ready{n}") for n in range(NC)]
        s_ready = [sem(f"s_ready{n}") for n in range(NC - 1)]
        NW = 26

        def run(eng, step):
            step(0)
            with eng.Fori(1, NPAIR) as t:
                step(t)

        def freed(eng, name, value):
            if not (isinstance(value, int) and value <= 0):
                eng.wait_ge(s[name], value)

        block = ctx.enter_context(nc.Block())
        x_d = x.rearrange("b (u p) d -> p (b u) d", p=P)
        out_d = out.rearrange("b (u p) d -> p (b u) d", p=P)

        @block.sync
        def _(sp):
            for i in range(NPAIR):
                sp.dma_start(x_sb[:, NT * i:NT * i + NT, :], x_d[:, NT * i:NT * i + NT, :]).then_inc(s["x_loaded"], 16)
            n = 0
            for dst, src in ((wv_sb[:], wvT), (wq_sb[:], wqT), (wk_sb[:], wkT), (wb_sb[:], wbT), (fs_sb[:], fsw),
                             (w1x[:], w1xT), (wo_sb[:], woT), (wg_sb[:], wg),
                             (b1_sb[:], b1),
                             (w2r[:], w2T.rearrange("(m p) n -> p m n", p=P)),
                             (w11_sb[:], w11.rearrange("e d f -> d e f")),
                             (w12_sb[:], w12.rearrange("e d f -> d e f")),
                             (w2_sb[:], w2.rearrange("e (c p) d -> p (e c) d", p=P)),
                             (on_sb[:], onw.partition_broadcast(P))):
                sp.dma_start(dst, src).then_inc(s["w_loaded"], 16)
                n += 1
            for k, w in enumerate((qcw, kcw, vcw)):
                sp.dma_start(taps[:, k, :, :], w.partition_broadcast(P)).then_inc(s["w_loaded"], 16)
                n += 1
            for h in range(H):
                q = slice(C * h, C * h + C)
                sp.dma_start(temp[q, 0:1], ltemp[h:h + 1].partition_broadcast(C)).then_inc(s["w_loaded"], 16)
                sp.dma_start(bias_hc[q, :], bbias[h, :].partition_broadcast(C)).then_inc(s["w_loaded"], 16)
                n += 2
            assert n == 25
            for h in range(H):
                q = slice(C * h, C * h + C)
                sp.dma_start(floor_hc[q, :], froor[h, :].partition_broadcast(C)).then_inc(s["w_loaded"], 16)
            sp.wait_ge(s["padw_ready"], 1)
            sp.dma_start(shear_d.rearrange("s (g c) k -> (s g) (c k)", g=4), toep_room[:, :]).then_inc(s["pw_stored"], 16)
            sp.wait_ge(s["pw_stored"], 16)
            sheared = bass.AP(shear_d.tensor, 0, [[D * LAGS * C + 1, C], [LAGS * C, D], [1, KL]])
            sp.dma_start(sheared, flr.partition_broadcast(C)).then_inc(s["pw_stored"], 16)
            sp.wait_ge(s["padw_ready"], 3)
            for h in range(H):
                for p in range(NP):
                    sp.dma_start(w1s[C * h + 2 * p:C * h + 2 * p + 2, :],
                                 w1sT[8 * p + 2 * h:8 * p + 2 * h + 2, :]).then_inc(s["w_loaded"], 16)
            sp.dma_start(t_d.rearrange("m p j -> p m j"), t16[:, :, :]).then_inc(s["t_zeroed"], 16)
            sp.wait_ge(s["pw_stored"], 32)
            for h in range(H):
                sp.dma_start(toep[C * h:C * h + C, :, :],
                             shear_d[:, C * h:C * h + C, :]).then_inc(s["toep_loaded"], 16)
            sp.wait_ge(s["t_zeroed"], 16)

            def pair(t):
                sp.wait_ge(s["a_ready"], t + 1)
                sp.dma_start(a_d.rearrange("m p j -> p m j"), a_hc[:, :, :]).then_inc(s["a_stored"], 16)
                sp.wait_ge(s["a_stored"], t * 16 + 16)
                blocks = a_d.rearrange("m (h k i) j -> k (m h) i j", h=H, k=2)
                for k in range(2):
                    sp.dma_start(a_it[64 * k:64 * k + 64, :, :],
                                 blocks[k, :, :, HB * k:HB * k + HB]).then_inc(s["a_items"], 16)
                sp.wait_ge(s["t_items"], t + 1)
                tblocks = t_d.rearrange("m (h k i) j -> k (m h) i j", h=H, k=2)
                for k in range(2):
                    sp.dma_start(tblocks[k, :, :, HB * k:HB * k + HB],
                                 t_it[64 * k:64 * k + 64, :, :]).then_inc(s["t_stored"], 16)
                sp.wait_ge(s["t_stored"], t * 32 + 32)
                sp.dma_start(t16[:, :, :], t_d.rearrange("m p j -> p m j")).then_inc(s["t16_loaded"], 16)

            run(sp, pair)

        @block.gpsimd
        def _(pool):
            count = [0]

            def link(ins):
                count[0] += 1
                ins.then_inc(s["pool_consts"], 1)
                pool.wait_ge(s["pool_consts"], count[0])

            pool.memset(toep_room[:], 0.0).then_inc(s["padw_ready"], 1)
            for z in (xnp[:, :, 0:KS], v_hc[:, :, 0:2, :], vf[:, :, 0:2]):
                pool.memset(z, 0.0).then_inc(s["pads_zero"], 1)
            pool.memset(t16[:], 0.0).then_inc(s["padw_ready"], 1)
            pool.memset(w1s[:], 0.0).then_inc(s["padw_ready"], 1)
            for z, v in ((ones, 1.0), (neg_low, -1.0), (keep_up, 1.0), (off_up, 1.0), (before, 1.0), (after, 1.0),
                         (id16, 1.0)):
                link(pool.memset(z[:], v))
            pool.memset(mh[:], -0.5).then_inc(s["consts_ready"], 1)
            pool.memset(w2e[:], 0.0).then_inc(s["consts_ready"], 1)
            link(pool.affine_select(out=ident[:], in_=ones[:], compare_op=ALU.is_equal, fill=0.0, base=0,
                                    pattern=[[-1, P]], channel_multiplier=1))
            for h in range(H):
                q = slice(C * h, C * h + C)
                link(pool.affine_select(out=neg_low[q, :], in_=neg_low[q, :], compare_op=ALU.is_gt, fill=0.0,
                                        base=0, pattern=[[-1, C]], channel_multiplier=1))
                link(pool.affine_select(out=keep_up[q, :], in_=keep_up[q, :], compare_op=ALU.is_ge, fill=0.0,
                                        base=0, pattern=[[1, C]], channel_multiplier=-1))
                link(pool.affine_select(out=off_up[q, :], in_=off_up[q, :], compare_op=ALU.is_ge, fill=0.0,
                                        base=HB - 1, pattern=[[0, C]], channel_multiplier=-1))
                link(pool.affine_select(out=off_up[q, :], in_=off_up[q, :], compare_op=ALU.is_ge, fill=0.0,
                                        base=-HB, pattern=[[1, C]], channel_multiplier=0))
            link(pool.affine_select(out=before[:], in_=before[:], compare_op=ALU.is_gt, fill=0.0, base=0,
                                    pattern=[[1, E], [-1, E]], channel_multiplier=0))
            link(pool.affine_select(out=after[:], in_=after[:], compare_op=ALU.is_gt, fill=0.0, base=0,
                                    pattern=[[-1, E], [1, E]], channel_multiplier=0))
            link(pool.affine_select(out=id16[:], in_=id16[:], compare_op=ALU.is_equal, fill=0.0, base=0,
                                    pattern=[[1, HB], [-1, HB]], channel_multiplier=0))
            pool.memset(st[:, 3, :], 0.0).then_inc(s["consts_ready"], 1)

            def v_pass(t):
                pool.wait_ge(s["ln_ms"], t + 1)
                pool.tensor_tensor(st[:, 2, 0:NT], st[:, 1, 0:NT], mh[:, 0:NT], ALU.pow).then_inc(s["ln_rs"], 1)

            run(pool, v_pass)

            def pair(t):
                done = [0]

                def chain(ins):
                    done[0] += 1
                    ins.then_inc(s["a_pool"], 1)
                    pool.wait_ge(s["a_pool"], t * A_POOL + done[0])

                pool.wait_ge(s["ms_ready"], t + 1)
                pool.tensor_tensor(rn[:, :, :], ss[:, :, :], mh[:, 0:2 * M].rearrange("p (a m) -> p a m", a=2),
                                   ALU.pow).then_inc(s["rn_ready"], 1)
                pool.wait_ge(s["beta_ready"], t + 1)
                pool.tensor_tensor(nbm[:, :, :], beta[:, :, :], neg_low[:, :].unsqueeze(1).to_broadcast([P, M, C]),
                                   ALU.mult).then_inc(s["nbm_ready"], 1)
                pool.wait_ge(s["at_ready"], t + 1)
                pool.tensor_tensor(a_off_t[:, :, :], a_t[:, :, :], off_up[:, :].unsqueeze(1).to_broadcast([P, M, C]),
                                   ALU.mult).then_inc(s["aoff_ready"], 1)
                pool.wait_ge(s["a_items"], t * 32 + 32)
                freed(pool, "t_stored", t * 32)
                chain(pool.tensor_tensor(t_it[:, :, :], a_it[:, :, :], id16[:, :, :], ALU.add))
                for j in range(1, HB - 1):
                    n = HB - 1 - j
                    pj = prod[:, 0:n * j].rearrange("p (i k) -> p i k", k=j)
                    chain(pool.tensor_tensor(pj, a_it[:, j + 1:HB, j:j + 1].to_broadcast([P, n, j]),
                                             t_it[:, j:j + 1, 0:j].to_broadcast([P, n, j]), ALU.mult))
                    ins = pool.tensor_tensor(t_it[:, j + 1:HB, 0:j], t_it[:, j + 1:HB, 0:j], pj, ALU.add)
                    if j < HB - 2:
                        chain(ins)
                    else:
                        ins.then_inc(s["t_items"], 1)
                pool.wait_ge(s["om_ready"], t + 1)
                pool.tensor_tensor(g1[:, :], g0[:, :], mh[:, 0:M], ALU.pow).then_inc(s["orn_ready"], 1)
                pool.wait_ge(s["b_ms"], t + 1)
                pool.tensor_tensor(st2[:, 2, :], st2[:, 1, :], mh[:, 0:NT], ALU.pow).then_inc(s["b_rs"], 1)
                assert done[0] == A_POOL, done[0]

            run(pool, pair)

        @block.tensor
        def _(pe):
            def heads(bank, col, n, lhs, rhs, **kw):
                for h in range(H):
                    q = slice(C * h, C * h + C)
                    ins = pe.matmul(bank[q, col:col + n], lhs(q), rhs(q), skip_group_check=True, **kw)
                return ins

            def held():
                pe.wait_ge(s["consts_ready"], 3)

            pe.wait_ge(s["pool_consts"], 27)
            def v_pass(t):
                pe.wait_ge(s["xn_ready"], t + 1)
                for j in range(NT):
                    ins = pe.transpose(ps[0][:, P * j:P * j + P], cen[:, j, :], ident[:, :])
                ins.then_inc(s["xt_done"], 1)
                pe.wait_ge(s["vp_vec"], 12)
                pe.wait_ge(s["xt_copied"], t + 1)
                for k in range(4):
                    ins = pe.matmul(ps[1][:, :], wvc[:, k, :], xnp[:, bass.ds(t * 2, 2), k:k + L],
                                    start=(k == 0), stop=(k == 3))
                ins.then_inc(s["v_proj"], 1)

            run(pe, v_pass)
            pe.wait_ge(s["v_copied"], NPAIR)
            pe.wait_ge(s["toep_loaded"], 64)
            pe.wait_ge(s["v_silu"], NPAIR)
            for c in range(DH):
                for lag in range(LAGS):
                    ins = heads(ps[2 + c // 8], c % 8 * B * NC, B * NC,
                                lambda q: toep[q, c, C * lag:C * lag + C],
                                lambda q: v_hc[q, :, 2 - lag:2 - lag + NC, c],
                                start=(lag == 0), stop=(lag == LAGS - 1))
                if c % 8 == 7:
                    ins.then_inc(s["fir_done"], 1)

            pe.wait_ge(s["long_ready"], 4)
            def pair(t):
                def chunks(bank, n, lhs, rhs):
                    for m in range(M):
                        ins = heads(bank(m), 0 if n is None else n * m % 512, n,
                                    lambda q: lhs(q, m), lambda q: rhs(q, m), start=True, stop=True)
                    return ins

                x_now = xnp[:, bass.ds(t * 2, 2), KS:KS + L]
                t1, t_16 = (t + 1, t * 16 + 16) if isinstance(t, int) else (pe.snap(t + 1), pe.snap(t * 16 + 16))
                pe.wait_ge(s["xn_ready"], t1)
                pe.wait_ge(s["w_loaded"], t_16)
                freed(pe, "x1_ready", t)
                for bank, w in ((0, wqc), (1, wkc)):
                    for k in range(4):
                        pe.matmul(ps[bank][:, :], w[:, k, :], xnp[:, bass.ds(t * 2, 2), k:k + L],
                                  start=(k == 0), stop=(k == 3))
                pe.matmul(ps[2][:, :], wbe[:, :, :], x_now, start=True, stop=True).then_inc(s["qkb_done"], 1)
                held()
                pe.wait_ge(s["kq_ready"], t1)
                pe.wait_ge(s["b_tanh"], t1)
                chunks(lambda m: ps[m // 8], 64, lambda q, m: kq_t[q, 0, m, :],
                       lambda q, m: kq_t[q, :, m, :]).then_inc(s["g_done"], 1)
                held()
                pe.wait_ge(s["aoff_ready"], t1)
                pe.wait_ge(s["t16_loaded"], t_16)
                chunks(lambda m: ps[2], 32, lambda q, m: a_off_t[q, m, :],
                       lambda q, m: t16[q, m, :]).then_inc(s["y_done"], 1)
                held()
                pe.wait_ge(s["y_ready"], t1)
                pe.wait_ge(s["t16t_ready"], t1)
                pe.wait_ge(s["attn_ready"], t1)
                chunks(lambda m: ps[0], 32, lambda q, m: y_sb[q, m, :],
                       lambda q, m: t16_t[q, m, :]).then_inc(s["t32_done"], 1)
                held()
                pe.wait_ge(s["t32_ready"], t1)
                pe.wait_ge(s["kbvb_ready"], t1)
                chunks(lambda m: ps[1], 32, lambda q, m: kb[q, m, :],
                       lambda q, m: t32_t[q, m, :]).then_inc(s["w_done"], 1)
                for n in range(NC):
                    held()
                    if n == 0:
                        pe.wait_ge(s["w_ready"], t1)
                    else:
                        pe.wait_ge(s_ready[n - 1], t1)
                    for b in range(2):
                        m = b * NC + n
                        ins = heads(ps[2], DH * b, DH, lambda q: t32_t[q, m, :], lambda q: vb[q, m, :],
                                    start=True, stop=(n == 0))
                        if n:
                            ins = heads(ps[2], DH * b, DH, lambda q: wneg_t[q, m, :], lambda q: s_sb[q, b, :],
                                        start=False, stop=True)
                    ins.then_inc(s["u_done"], 1)
                    held()
                    pe.wait_ge(u_ready[n], t1)
                    if n < NC - 1:
                        for b in range(2):
                            m = b * NC + n
                            ins = heads(ps[1], DH * b, DH, lambda q: kn[q, m, :], lambda q: u_sb[q, b, :],
                                        start=(n == 0 and b == 0), stop=(n == NC - 2))
                        ins.then_inc(s["s_done"], 1)
                    for b in range(2):
                        m = b * NC + n
                        if n:
                            heads(ps[0], DH * m, DH, lambda q: kq_t[q, 1, m, :], lambda q: s_sb[q, b, :],
                                  start=True, stop=False)
                        ins = heads(ps[0], DH * m, DH, lambda q: attn_t[q, m, :], lambda q: u_sb[q, b, :],
                                    start=(n == 0), stop=True)
                    ins.then_inc(s["o_done"], 1)
                pe.wait_ge(s["stats_ready"], t + 1)
                for k in range(2):
                    pe.matmul(ps[k][:, :], w1x[:, P * k:P * k + P], x_now, start=True, stop=False)
                    pe.matmul(ps[k][:, :], w1s[:, P * k:P * k + P], stats_t[:, :, :].rearrange("p m t -> p (m t)"),
                              start=False, stop=True).then_inc(s["hmid_done"], 1)
                pe.wait_ge(s["hm_ready"], t * 2 + 2)
                for k in range(2):
                    ins = pe.matmul(ps[2][:, :], w2e[:, k, :, :].rearrange("p h j -> p (h j)"), hm[:, k, :],
                                    start=(k == 0), stop=(k == 1))
                ins.then_inc(s["lg_done"], 1)
                pe.wait_ge(s["ot_ready"], t + 1)
                for j in range(NT):
                    ins = pe.matmul(ps[0][:, P * j:P * j + P], o_t[:, P * j:P * j + P], wo_sb[:, :],
                                    start=True, stop=True)
                ins.then_inc(s["wo_done"], 1)

                pe.wait_ge(s["xn2_ready"], t + 1)
                freed(pe, "acc_done", t * E)
                for j in range(NT):
                    ins = pe.transpose(ps[7][:, P * j:P * j + P], cen2[:, j, :], ident[:, :])
                ins.then_inc(s["x2t_done"], 1)
                pe.wait_ge(s["x2t_ready"], t + 1)
                for j in range(NT):
                    ins = pe.matmul(ps[7][:, E * j:E * j + E], x2t[:, P * j:P * j + P], wg_sb[:, :],
                                    start=True, stop=True)
                ins.then_inc(s["r_done"], 1)
                for e in range(E + 1):
                    for f in range(FC if e < E else 0):
                        i = FC * e + f
                        if i >= 2:
                            pe.wait_ge(s["fu_ready"], t * E * FC + i - 1)
                        for bank, w, done in ((3, w11_sb, "gate_done"), (5, w12_sb, "val_done")):
                            pe.matmul(ps[bank + i % 2][:, :], w[:, e, P * f:P * f + P], x2t[:, :],
                                      start=True, stop=True).then_inc(s[done], 1)
                    if e >= 1:
                        pe.wait_ge(s["fu_ready"], t * E * FC + FC * e)
                        if e == 1:
                            pe.wait_ge(s["r_in"], t + 1)
                        else:
                            pe.wait_ge(s["acc_done"], t * E + e - 1)
                        for j in range(NT):
                            for f in range(FC):
                                ins = pe.matmul(ps[7][:, P * j:P * j + P], fu[:, (e - 1) % 2, f, P * j:P * j + P],
                                                w2_sb[:, FC * (e - 1) + f, :], start=(f == 0), stop=(f == FC - 1))
                        ins.then_inc(s["y2_done"], 1)

            run(pe, pair)

        @block.scalar
        def _(act):
            def v_pass(t):
                act.wait_ge(s["vp_vec"], t * V_VEC + 14)
                act.activation(sq[:, :, :], cen[:, :, :], ACT.Square).then_inc(s["ln_sq"], 1)
                act.wait_ge(s["pads_zero"], 3)
                act.wait_ge(s["xt_done"], t + 1)
                act.activation(xnp[:, bass.ds(t * 2, 2), KS:KS + L], ps[0][:, :].rearrange("p (b l) -> p b l", b=2),
                               ACT.Copy).then_inc(s["xt_copied"], 1)
                act.wait_ge(s["v_proj"], t + 1)
                freed(act, "vt_ready", t)
                freed(act, "sft_ready", t)
                act.activation(vf[:, :, 2:2 + L], ps[1][:, :].rearrange("p (b l) -> p b l", b=2),
                               ACT.Silu).then_inc(s["v_silu"], 1)
                act.wait_ge(s["vt_ready"], t + 1)
                act.activation(v_hc[:, bass.ds(t * 2, 2), 2:2 + NC, :].rearrange("p b n d -> p b (n d)"),
                               vt[:, :, :].rearrange("p (b n) d -> p b (n d)", b=2), ACT.Copy).then_inc(s["v_copied"], 1)
                act.wait_ge(s["sft_ready"], t + 1)
                act.activation(short_hc[:, bass.ds(t * M, M), :], sft[:, :, :], ACT.Copy).then_inc(s["s_copied"], 1)
            run(act, v_pass)
            act.wait_ge(s["w_loaded"], 16 * 45)
            act.activation(temp[:, 1:2], temp[:, 0:1], ACT.Abs).then_inc(s["vp_act"], 1)
            act.wait_ge(s["vp_act"], 1)
            act.activation(temp[:, 2:3], temp[:, 1:2], ACT.Exp, scale=-1.0).then_inc(s["vp_act"], 1)
            act.wait_ge(s["vp_act"], 2)
            act.activation(temp[:, 3:4], temp[:, 2:3], ACT.Ln, bias=1.0).then_inc(s["vp_act"], 1)
            act.activation(floor_hc[:, :], floor_hc[:, :], ACT.Sigmoid).then_inc(s["vp_act"], 1)
            for c in range(4):
                act.wait_ge(s["fir_done"], c + 1)
                act.activation(long_hc[:, :, 8 * c:8 * c + 8].rearrange("p m c -> p c m"),
                               ps[2 + c][:, :].rearrange("p (c m) -> p c m", c=8), ACT.Copy).then_inc(s["long_ready"], 1)

            act.wait_ge(s["v_copied"], NPAIR)
            act.wait_ge(s["s_copied"], NPAIR)
            act.wait_ge(s["long_ready"], 4)
            def pair(t):
                freed(act, "x1_ready", t)
                for p, src in ((0, short_hc), (1, long_hc)):
                    act.activation(paths[:, p, :, :], src[:, bass.ds(t * M, M), :], ACT.Copy).then_inc(s["p_copied"], 1)
                act.activation(paths[:, 3, :, :].rearrange("p (b n) d -> p b (n d)", b=2),
                               v_hc[:, bass.ds(t * 2, 2), 2:2 + NC, :].rearrange("p b n d -> p b (n d)"),
                               ACT.Copy).then_inc(s["p_copied"], 1)
                act.wait_ge(s["qkb_done"], t + 1)
                act.activation(tb[:, :, :], ps[2][:, :].rearrange("p (m t) -> p m t", m=M), ACT.Tanh,
                               scale=0.5).then_inc(s["b_tanh"], 1)
                act.activation(kf[:, :, :], ps[1][:, :].rearrange("p (m t) -> p m t", m=M),
                               ACT.Silu).then_inc(s["k_silu"], 1)
                act.activation(qf[:, :, :], ps[0][:, :].rearrange("p (m t) -> p m t", m=M),
                               ACT.Silu).then_inc(s["q_silu"], 1)
                act.wait_ge(s["qk_ready"], t * 2 + 2)
                act.activation(qk_sq[:, :, :, :], qk_hc[:, :, :, :], ACT.Square).then_inc(s["qk_squared"], 1)
                act.wait_ge(s["y_done"], t + 1)
                act.activation(y_sb[:, :, :], ps[2][:, :].rearrange("p (m t) -> p m t", m=M),
                               ACT.Copy).then_inc(s["y_ready"], 1)
                act.wait_ge(s["w_done"], t + 1)
                act.activation(wneg_t[:, :, :], ps[1][:, :].rearrange("p (m t) -> p m t", m=M), ACT.Copy,
                               scale=-1.0).then_inc(s["w_ready"], 1)
                for n in range(NC - 1):
                    act.wait_ge(s["s_done"], t * (NC - 1) + n + 1)
                    if n:
                        act.wait_ge(s["o_done"], t * NC + n + 1)
                    act.activation(s_sb[:, :, :], ps[1][:, 0:2 * DH].rearrange("p (b d) -> p b d", b=2),
                                   ACT.Copy).then_inc(s_ready[n], 1)
                act.wait_ge(s["o_done"], t * NC + NC)
                act.activation(paths[:, 2, :, :], ps[0][:, :].rearrange("p (m d) -> p m d", m=M),
                               ACT.Copy).then_inc(s["delta_ready"], 1)
                act.wait_ge(s["cen_ready"], t + 1)
                act.activation(psq[:, :, :, :], pcen[:, :, :, :], ACT.Square).then_inc(s["psq_ready"], 1)
                for k in range(2):
                    act.wait_ge(s["hmid_done"], t * 2 + k + 1)
                    act.activation(hm[:, k, :], ps[k][:, :], ACT.Gelu, bias=b1_sb[:, k:k + 1]).then_inc(s["hm_ready"], 1)
                act.wait_ge(s["ex_in"], t + 1)
                act.activation(pr[:, :, :], lb[:, :, :], ACT.Exp, scale=temp[:, 1:2]).then_inc(s["ex_out"], 1)
                act.wait_ge(s["mix_ready"], t + 1)
                act.activation(psq[:, 0, :, :], oh[:, :, :], ACT.Square).then_inc(s["osq_ready"], 1)

                act.wait_ge(s["b_cen"], t + 1)
                act.activation(sq2[:, :, :], cen2[:, :, :], ACT.Square).then_inc(s["b_sq"], 1)
                act.wait_ge(s["x2t_done"], t + 1)
                act.activation(x2t[:, :], ps[7][:, :], ACT.Copy).then_inc(s["x2t_ready"], 1)
                act.wait_ge(s["r_in"], t + 1)
                act.activation(rt[:, :, :], rs[:, :, :], ACT.Exp).then_inc(s["r_ex"], 1)
                for i in range(E * FC):
                    act.wait_ge(s["gate_done"], t * E * FC + i + 1)
                    if i >= 2:
                        act.wait_ge(s["fu_ready"], t * E * FC + i - 1)
                    act.activation(sg[:, i % 2, :], ps[3 + i % 2][:, :], ACT.Silu).then_inc(s["sg_ready"], 1)
                act.wait_ge(s["acc_done"], t * E + E)
                act.dma_start(out_d[:, bass.ds(t * NT, NT), :], x1[:, 0, :, :]).then_inc(s["out_stored"], 16)
            run(act, pair)
            act.wait_ge(s["out_stored"], 16 * NPAIR)

        @block.vector
        def _(dve):
            dve.wait_ge(s["w_loaded"], 16 * 45)
            for k, (dst, src) in enumerate(((wqc, wq_sb), (wkc, wk_sb), (wvc, wv_sb))):
                for j in range(4):
                    dve.tensor_tensor(dst[:, j, :], src[:, :], taps[:, k, j, :], ALU.mult).then_inc(s["vp_vec"], 1)
            dve.tensor_copy(wbe[:, :, :], wb_sb[:, :].unsqueeze(2).to_broadcast([P, H, C])).then_inc(s["wb_expanded"], 1)
            dve.wait_ge(s["consts_ready"], 3)
            dve.tensor_copy(w2e[:, :, :, 0:NP], w2r[:, :, :].rearrange("p k (h j) -> p k h j", h=H)).then_inc(s["wb_expanded"], 1)
            base = 12
            def v_pass(t):
                done = [0]

                def chain(ins):
                    done[0] += 1
                    ins.then_inc(s["vp_vec"], 1)
                    dve.wait_ge(s["vp_vec"], t * V_VEC + base + done[0])

                dve.wait_ge(s["x_loaded"], 64)
                freed(dve, "xt_done", t)
                freed(dve, "ln_sq", t)
                xt = x_sb[:, bass.ds(t * NT, NT), :]
                chain(dve.tensor_reduce(st[:, 0, 0:NT], xt, AX.X, ALU.add))
                dve.scalar_tensor_tensor(cen[:, :, :], st[:, 0, 0:NT].unsqueeze(2).to_broadcast([P, NT, D]),
                                         -1.0 / D, xt, ALU.mult, ALU.add).then_inc(s["vp_vec"], 1)
                done[0] += 1
                dve.wait_ge(s["ln_sq"], t + 1)
                chain(dve.tensor_reduce(st[:, 1, 0:NT], sq[:, :, :], AX.X, ALU.add))
                dve.tensor_scalar(st[:, 1, 0:NT], st[:, 1, 0:NT], 1.0 / D, 1e-5, ALU.mult,
                                  ALU.add).then_inc(s["ln_ms"], 1)
                dve.wait_ge(s["ln_rs"], t + 1)
                dve.tensor_tensor(cen[:, :, :], cen[:, :, :], st[:, 2, 0:NT].unsqueeze(2).to_broadcast([P, NT, D]),
                                  ALU.mult).then_inc(s["xn_ready"], 1)
                dve.wait_ge(s["pads_zero"], 3)
                dve.wait_ge(s["v_silu"], t + 1)
                freed(dve, "v_copied", t)
                for b in range(2):
                    ins = dve.transpose(vt[:, NC * b:NC * b + NC, :].rearrange("p n c -> p (n c)"), vf[:, b, 2:2 + L])
                    if b == 0:
                        chain(ins)
                    else:
                        ins.then_inc(s["vt_ready"], 1)
                freed(dve, "s_copied", t)
                chain(dve.tensor_scalar(sf0[:, :, :], vf[:, :, 0:L], fs_sb[:, 0:1], None, ALU.mult))
                chain(dve.scalar_tensor_tensor(sf1[:, :, :], vf[:, :, 1:1 + L], fs_sb[:, 1:2], sf0[:, :, :],
                                               ALU.mult, ALU.add))
                chain(dve.scalar_tensor_tensor(sf0[:, :, :], vf[:, :, 2:2 + L], fs_sb[:, 2:3], sf1[:, :, :],
                                               ALU.mult, ALU.add))
                chain(dve.tensor_scalar(st[:, 3, 0:1], st[:, 3, 0:1], 0.0, None, ALU.mult))
                dve.transpose(sft[:, :, :].rearrange("p m c -> p (m c)"),
                              sf0[:, :, :].rearrange("p b l -> p (b l)")).then_inc(s["sft_ready"], 1)
                assert done[0] == V_VEC, done[0]

            run(dve, v_pass)
            dve.wait_ge(s["vp_act"], 4)
            base += V_VEC * NPAIR
            lone = [base]

            def step(ins):
                lone[0] += 1
                ins.then_inc(s["vp_vec"], 1)
                dve.wait_ge(s["vp_vec"], lone[0])

            step(dve.tensor_scalar(temp[:, 0:1], temp[:, 0:1], 0.0, None, ALU.max))
            step(dve.tensor_tensor(temp[:, 0:1], temp[:, 0:1], temp[:, 3:4], ALU.add))
            step(dve.tensor_scalar(temp[:, 0:1], temp[:, 0:1], 1e-4, None, ALU.add))
            step(dve.reciprocal(temp[:, 1:2], temp[:, 0:1]))
            step(dve.tensor_scalar(floor_hc[:, :], floor_hc[:, :], 0.05, None, ALU.mult))

            dve.wait_ge(s["pool_consts"], 27)
            dve.memset(stats[:], 0.0).then_inc(s["sm_exp0"], 1)
            dve.wait_ge(s["sm_exp0"], 1)
            dve.wait_ge(s["long_ready"], 4)
            def pair(t):
                na, nb = [0], [0]

                def chain(ins):
                    na[0] += 1
                    ins.then_inc(s["a_vec"], 1)
                    dve.wait_ge(s["a_vec"], t * A_VEC + na[0])

                def chain_b(ins):
                    nb[0] += 1
                    ins.then_inc(s["b_vec"], 1)
                    dve.wait_ge(s["b_vec"], t * B_VEC + nb[0])

                def flat(a):
                    return a.rearrange("p m c -> p (m c)")

                dve.wait_ge(s["b_tanh"], t + 1)
                chain(dve.transpose(flat(bt[:, :, :]), flat(tb[:, :, :])))
                dve.tensor_scalar(beta[:, :, :], bt[:, :, :], 0.5, 0.5, ALU.mult, ALU.add).then_inc(s["beta_ready"], 1)
                dve.wait_ge(s["k_silu"], t + 1)
                dve.transpose(flat(qk_hc[:, 1, :, :]), flat(kf[:, :, :])).then_inc(s["qk_ready"], 1)
                dve.wait_ge(s["q_silu"], t + 1)
                dve.transpose(flat(qk_hc[:, 0, :, :]), flat(qf[:, :, :])).then_inc(s["qk_ready"], 1)
                dve.wait_ge(s["beta_ready"], t + 1)
                chain(
                    dve.tensor_tensor(vb[:, :, :].rearrange("p (b n) d -> p b (n d)", b=2),
                                      v_hc[:, bass.ds(t * 2, 2), 2:2 + NC, :].rearrange("p b n d -> p b (n d)"),
                                      beta[:, :, :].rearrange("p (b n) d -> p b (n d)", b=2), ALU.mult))
                dve.wait_ge(s["qk_squared"], t + 1)
                chain(dve.tensor_reduce(ss[:, :, :], qk_sq[:, :, :, :], AX.X, ALU.add))
                dve.tensor_scalar(ss[:, :, :], ss[:, :, :], 1e-6, None, ALU.add).then_inc(s["ms_ready"], 1)
                dve.wait_ge(s["rn_ready"], t + 1)
                chain(dve.tensor_tensor(kn[:, :, :], qk_hc[:, 1, :, :], rn[:, 1, :].unsqueeze(2).to_broadcast([P, M, DH]),
                                        ALU.mult))
                chain(dve.tensor_tensor(qn[:, :, :], qk_hc[:, 0, :, :], rn[:, 0, :].unsqueeze(2).to_broadcast([P, M, DH]),
                                        ALU.mult))
                chain(dve.transpose(flat(kq_t[:, 0, :, :]), flat(kn[:, :, :])))
                dve.transpose(flat(kq_t[:, 1, :, :]), flat(qn[:, :, :])).then_inc(s["kq_ready"], 1)
                dve.tensor_tensor(kb[:, :, :], kn[:, :, :], beta[:, :, :], ALU.mult).then_inc(s["kbvb_ready"], 1)
                dve.wait_ge(s["g_done"], t + 1)
                dve.wait_ge(s["nbm_ready"], t + 1)
                for k in range(2):
                    g = ps[k][:, :].rearrange("p (m a j) -> p m a j", m=8, a=2)
                    ins = dve.tensor_tensor(a_hc[:, 8 * k:8 * k + 8, :], g[:, :, 0, :], nbm[:, 8 * k:8 * k + 8, :],
                                            ALU.mult)
                    if k == 0:
                        chain(ins)
                    else:
                        ins.then_inc(s["a_ready"], 1)
                dve.wait_ge(s["a_ready"], t + 1)
                dve.transpose(flat(a_t[:, :, :]), flat(a_hc[:, :, :])).then_inc(s["at_ready"], 1)
                for k in range(2):
                    g = ps[k][:, :].rearrange("p (m a j) -> p m a j", m=8, a=2)
                    ins = dve.tensor_tensor(attn_t[:, 8 * k:8 * k + 8, :], g[:, :, 1, :],
                                            keep_up[:, :].unsqueeze(1).to_broadcast([P, 8, C]), ALU.mult)
                    if k == 0:
                        chain(ins)
                    else:
                        ins.then_inc(s["attn_ready"], 1)
                dve.wait_ge(s["t16_loaded"], t * 16 + 16)
                dve.transpose(flat(t16_t[:, :, :]), flat(t16[:, :, :])).then_inc(s["t16t_ready"], 1)
                dve.wait_ge(s["t16t_ready"], t + 1)
                dve.wait_ge(s["t32_done"], t + 1)
                dve.tensor_tensor(t32_t[:, :, :], ps[0][:, :].rearrange("p (m t) -> p m t", m=M), t16_t[:, :, :],
                                  ALU.add).then_inc(s["t32_ready"], 1)
                for n in range(NC):
                    dve.wait_ge(s["u_done"], t * NC + n + 1)
                    if n:
                        dve.wait_ge(s["o_done"], t * NC + n)
                    dve.tensor_copy(u_sb[:, :, :], ps[2][:, 0:2 * DH].rearrange("p (b d) -> p b d", b=2)).then_inc(
                        u_ready[n], 1)
                dve.wait_ge(s["p_copied"], t * 3 + 3)
                dve.wait_ge(s["delta_ready"], t + 1)
                chain(dve.tensor_reduce(psum_[:, :, :], paths[:, :, :, :], AX.X, ALU.add))
                chain(dve.tensor_scalar(psum_[:, :, :], psum_[:, :, :], 1.0 / DH, None, ALU.mult))
                fp = "p a m d -> p (a m) d"
                dve.tensor_tensor(pcen[:, :, :, :].rearrange(fp), paths[:, :, :, :].rearrange(fp),
                                  psum_[:, :, :].rearrange("p a m -> p (a m)").unsqueeze(2).to_broadcast([P, NP * M, DH]),
                                  ALU.subtract).then_inc(s["cen_ready"], 1)
                chain(dve.tensor_copy(stats[:, :, 0:8:2].rearrange("p m a -> p a m"), psum_[:, :, :]))
                dve.wait_ge(s["psq_ready"], t + 1)
                chain(dve.tensor_reduce(pvar[:, :, :], psq[:, :, :, :], AX.X, ALU.add))
                chain(dve.tensor_scalar(stats[:, :, 1:8:2].rearrange("p m a -> p a m"), pvar[:, :, :], 1.0 / DH, None,
                                        ALU.mult))
                dve.transpose(flat(stats_t[:, :, :]), flat(stats[:, :, :])).then_inc(s["stats_ready"], 1)
                dve.wait_ge(s["lg_done"], t + 1)
                chain(dve.transpose(flat(lg[:, :, :]), ps[2][:, :]))
                chain(dve.tensor_tensor(lb[:, :, :], lg[:, :, 0:NP], bias_hc[:, :].unsqueeze(1).to_broadcast([P, M, NP]),
                                        ALU.add))
                chain(dve.tensor_reduce(g0[:, :], lb[:, :, :], AX.X, ALU.max))
                dve.tensor_tensor(lb[:, :, :], lb[:, :, :], g0[:, :].unsqueeze(2).to_broadcast([P, M, NP]),
                                  ALU.subtract).then_inc(s["ex_in"], 1)
                dve.wait_ge(s["ex_out"], t + 1)
                for again in range(2):
                    chain(dve.tensor_reduce(g0[:, :], pr[:, :, :], AX.X, ALU.add))
                    chain(dve.reciprocal(g0[:, :], g0[:, :]))
                    chain(dve.tensor_tensor(pr[:, :, :], pr[:, :, :], g0[:, :].unsqueeze(2).to_broadcast([P, M, NP]),
                                            ALU.mult))
                    if not again:
                        chain(dve.tensor_tensor(pr[:, :, :], pr[:, :, :],
                                                floor_hc[:, :].unsqueeze(1).to_broadcast([P, M, NP]), ALU.max))
                for p in range(NP):
                    ins = dve.tensor_tensor(pcen[:, p, :, :], paths[:, p, :, :],
                                            pr[:, :, p:p + 1].to_broadcast([P, M, DH]), ALU.mult)
                    if p == NP - 1:
                        chain(ins)
                chain(dve.tensor_tensor(pcen[:, 0:2, :, :], pcen[:, 0:2, :, :], pcen[:, 2:4, :, :], ALU.add))
                dve.tensor_tensor(oh[:, :, :], pcen[:, 0, :, :], pcen[:, 1, :, :], ALU.add).then_inc(s["mix_ready"], 1)
                dve.wait_ge(s["osq_ready"], t + 1)
                chain(dve.tensor_reduce(g0[:, :], psq[:, 0, :, :], AX.X, ALU.add))
                dve.tensor_scalar(g0[:, :], g0[:, :], 1.0 / DH, 1e-5, ALU.mult, ALU.add).then_inc(s["om_ready"], 1)
                dve.wait_ge(s["orn_ready"], t + 1)
                chain(dve.tensor_tensor(oh[:, :, :], oh[:, :, :], g1[:, :].unsqueeze(2).to_broadcast([P, M, DH]),
                                        ALU.mult))
                chain(dve.tensor_tensor(oh[:, :, :], oh[:, :, :], on_sb[:, :].unsqueeze(1).to_broadcast([P, M, DH]),
                                        ALU.mult))
                dve.transpose(o_t[:, :], flat(oh[:, :, :])).then_inc(s["ot_ready"], 1)
                dve.wait_ge(s["wo_done"], t + 1)
                freed(dve, "out_stored", t * 16)
                dve.tensor_tensor(x1[:, 0, :, :], ps[0][:, :].rearrange("p (j d) -> p j d", j=NT),
                                  x_sb[:, bass.ds(t * NT, NT), :], ALU.add).then_inc(s["x1_ready"], 1)
                assert na[0] == A_VEC, na[0]

                dve.wait_ge(s["x1_ready"], t + 1)
                chain_b(dve.tensor_reduce(st2[:, 0, :], x1[:, 0, :, :], AX.X, ALU.add))
                dve.scalar_tensor_tensor(cen2[:, :, :], st2[:, 0, :].unsqueeze(2).to_broadcast([P, NT, D]), -1.0 / D,
                                         x1[:, 0, :, :], ALU.mult, ALU.add).then_inc(s["b_cen"], 1)
                dve.wait_ge(s["b_sq"], t + 1)
                chain_b(dve.tensor_reduce(st2[:, 1, :], sq2[:, :, :], AX.X, ALU.add))
                dve.tensor_scalar(st2[:, 1, :], st2[:, 1, :], 1.0 / D, 1e-5, ALU.mult, ALU.add).then_inc(s["b_ms"], 1)
                dve.wait_ge(s["b_rs"], t + 1)
                dve.tensor_tensor(cen2[:, :, :], cen2[:, :, :], st2[:, 2, :].unsqueeze(2).to_broadcast([P, NT, D]),
                                  ALU.mult).then_inc(s["xn2_ready"], 1)
                dve.wait_ge(s["r_done"], t + 1)
                chain_b(dve.tensor_reduce(st2[:, 3, :], ps[7][:, 0:NT * E].rearrange("p (j e) -> p j e", e=E), AX.X,
                                          ALU.max))
                dve.tensor_tensor(rs[:, :, :], ps[7][:, 0:NT * E].rearrange("p (j e) -> p j e", e=E),
                                  st2[:, 3, :].unsqueeze(2).to_broadcast([P, NT, E]), ALU.subtract).then_inc(s["r_in"], 1)

                def weigh():
                    dve.wait_ge(s["r_ex"], t + 1)
                    chain_b(dve.tensor_reduce(st2[:, 3, :], rt[:, :, :], AX.X, ALU.add))
                    chain_b(dve.reciprocal(st2[:, 3, :], st2[:, 3, :]))
                    chain_b(dve.tensor_tensor(rt[:, :, :], rt[:, :, :], st2[:, 3, :].unsqueeze(2).to_broadcast([P, NT, E]),
                                              ALU.mult))
                    for j in range(NT):
                        of = rt[:, j:j + 1, :].to_broadcast([P, E, E])
                        oe = rt[:, j, :].unsqueeze(2).to_broadcast([P, E, E])
                        dve.tensor_tensor(cmp[:, j, :, :], of, oe, ALU.is_ge)
                        ins = dve.tensor_tensor(cmq[:, j, :, :], of, oe, ALU.is_gt)
                    chain_b(ins)
                    fl = "p j e f -> p j (e f)"
                    bc = [P, NT, E * E]
                    chain_b(dve.tensor_tensor(cmp[:, :, :, :].rearrange(fl), cmp[:, :, :, :].rearrange(fl),
                                              before[:, :, :].rearrange("p e f -> p (e f)").unsqueeze(1).to_broadcast(bc),
                                              ALU.mult))
                    chain_b(dve.tensor_tensor(cmq[:, :, :, :].rearrange(fl), cmq[:, :, :, :].rearrange(fl),
                                              after[:, :, :].rearrange("p e f -> p (e f)").unsqueeze(1).to_broadcast(bc),
                                              ALU.mult))
                    chain_b(dve.tensor_tensor(cmp[:], cmp[:], cmq[:], ALU.add))
                    chain_b(dve.tensor_reduce(ru[:, :, :], cmp[:, :, :, :], AX.X, ALU.add))
                    chain_b(dve.scalar_tensor_tensor(rs[:, :, :], ru[:, :, :], 1.5, rt[:, :, :], ALU.is_lt, ALU.mult))
                    chain_b(dve.tensor_reduce(st2[:, 3, :], rs[:, :, :], AX.X, ALU.add))
                    chain_b(dve.tensor_scalar(st2[:, 3, :], st2[:, 3, :], 1e-8, None, ALU.add))
                    chain_b(dve.reciprocal(st2[:, 3, :], st2[:, 3, :]))
                    chain_b(dve.tensor_tensor(rs[:, :, :], rs[:, :, :], st2[:, 3, :].unsqueeze(2).to_broadcast([P, NT, E]),
                                              ALU.mult))

                for e in range(E + 1):
                    for f in range(FC if e < E else 0):
                        i = FC * e + f
                        dve.wait_ge(s["sg_ready"], t * E * FC + i + 1)
                        dve.wait_ge(s["val_done"], t * E * FC + i + 1)
                        if e >= 2:
                            dve.wait_ge(s["y2_done"], t * E + e - 1)
                        dve.tensor_tensor(fu[:, e % 2, f, :], sg[:, i % 2, :], ps[5 + i % 2][:, :],
                                          ALU.mult).then_inc(s["fu_ready"], 1)
                    if e == 0:
                        weigh()
                    if e >= 1:
                        dve.wait_ge(s["y2_done"], t * E + e)
                        if e >= 2:
                            dve.wait_ge(s["acc_done"], t * E + e - 1)
                        for j in range(NT):
                            ins = dve.scalar_tensor_tensor(x1[:, 0, j, :], ps[7][:, P * j:P * j + P],
                                                           rs[:, j, e - 1:e], x1[:, 0, j, :], ALU.mult, ALU.add)
                        ins.then_inc(s["acc_done"], 1)
                assert nb[0] == B_VEC, nb[0]

            run(dve, pair)


_OUT = (B, L, D)


def kernel(**inputs):
    import numpy as np
    import concourse.bacc as bacc
    from concourse.bass_utils import run_bass_kernel_spmd

    a = {k.split("_", 2)[2]: np.asarray(v) for k, v in inputs.items()}
    w1T = a["gate_w1"].T
    laid = [("x", a["hidden_states"]), ("wqT", a["Wq"].T), ("wkT", a["Wk"].T), ("wvT", a["Wv"].T), ("wbT", a["Wb"].T),
            ("qcw", a["qconv_w"].T), ("kcw", a["kconv_w"].T), ("vcw", a["vconv_w"].T),
            ("fsw", a["fir_short_w"].reshape(D, KS)), ("flr", a["fir_long_w"].reshape(D, KL)[:, ::-1]),
            ("w1xT", w1T[:D]), ("w1sT", w1T[D:]), ("b1", a["gate_b1"].reshape(2, P).T), ("w2T", a["gate_w2"].T),
            ("ltemp", a["log_temp"]), ("bbias", a["base_bias"]), ("froor", a["floor_raw"]), ("onw", a["onorm_w"]),
            ("woT", a["Wo"].T), ("wg", a["Wg"]), ("w11", a["W11"]), ("w12", a["W12"]), ("w2", a["W2"])]
    nc = bacc.Bacc("TRN2", target_bir_lowering=False, num_devices=1)
    arrays, args = {}, []
    for name, v in laid:
        v = np.ascontiguousarray(v)
        arrays[f"in_{name}"] = v
        args.append(nc.dram_tensor(f"in_{name}", v.shape, mybir.dt.from_np(v.dtype), kind="ExternalInput").ap())
    args.append(nc.dram_tensor("out_y", _OUT, F32, kind="ExternalOutput").ap())
    build(nc, *args)
    r = run_bass_kernel_spmd(nc, [arrays], core_ids=[0])
    return r.results[0]["out_y"]
```

```python
from contextlib import ExitStack

import concourse.bass as bass
from concourse import mybir

F32 = mybir.dt.float32
ALU = mybir.AluOpType
ACT = mybir.ActivationFunctionType
AX = mybir.AxisListType

P = 128
B, L, D = 8, 256, 128
H, DH = 4, 32
C = 32
NPAIR = B // 2
TOK = 2 * L
NT = TOK // P
M = TOK // C
NC = L // C
HB = C // 2
KS, KL = 3, 63
LAGS = 3
NP = 4
HID = 256
E, FF = 8, 256
FC = FF // P

A1_VEC, A2_VEC, A1_POOL, B_VEC, V_VEC, V_POOL = 6, 18, 28, 16, 2, 4

PADS_READY, ALL_CONSTS = 6, 32

SLOTS = [[("gv", 0)], [("gv", 1)], [("g", 0)], [("g", 1)], [("y", 0)], [("gv", 2)], [("gv", 3)], [("y", 1)],
         [("gv", 4)], [("gv", 5)], [("y", 2)], [("gv", 6)], [("gv", 7)], [("y", 3)], [("gv", 8)], [("gv", 9)],
         [("y", 4), ("gv", 10), ("gv", 11), ("y", 5), ("gv", 12)], [("gv", 13)],
         [("y", 6), ("gv", 14), ("gv", 15), ("y", 7)]]


def build(nc, x, early, taps_row, late, flr, w11, w12, w2, out):
    ctx = ExitStack()
    with ctx:
        def sb(name, *shape):
            return ctx.enter_context(nc.sbuf_tensor(name, [P, *shape], F32))

        def sem(name):
            return ctx.enter_context(nc.semaphore(name))

        def parts(room, *widths):
            at = 0
            for w in widths:
                yield room[:, at:at + w]
                at += w

        x_sb = sb("x_sb", 2 * B, D)
        xnp = sb("xnp", B, KS + L)
        v_hc = sb("v_hc", B, 2 + NC, DH)
        short_hc = sb("short_hc", B * NC, DH)
        long_hc = sb("long_hc", B * NC, DH)
        toep_room = sb("toep_room", DH * LAGS * C)
        toep = toep_room[:, :].rearrange("p (c k) -> p c k", c=DH)
        early_sb = sb("early_sb", D + H + KS)
        wv_sb, wb_sb, fs_sb = parts(early_sb, D, H, KS)
        late_sb = sb("late_sb", 3 * D + 2 * HID + 2 + 2 * H * NP + E + 2 * NP + 1 + DH)
        (wq_sb, wk_sb, wo_sb, w1x, w1s, b1_sb, w2r, wg_sb, bias_hc, floor_hc, logt, on_sb) = parts(
            late_sb, D, D, D, HID, HID, 2, 2 * H * NP, E, NP, NP, 1, DH)
        taps_room = sb("taps_room", 3 * 4 * D)
        taps = taps_room[:, :].rearrange("p (k j d) -> p k j d", k=3, j=4)
        wqc, wkc, wvc = sb("wqc", 4, D), sb("wkc", 4, D), sb("wvc", 4, D)
        wbe = sb("wbe", H, C)
        w2e = sb("w2e", 2, H, C)
        w11_sb, w12_sb = sb("w11_sb", E, FF), sb("w12_sb", E, FF)
        w2_sb = sb("w2_sb", E * FC, D)
        temp = sb("temp", 4)
        ones, ident = sb("ones", P), sb("ident", P)
        neg_low = sb("neg_low", DH)
        keep_up = sb("keep_up", DH)
        off_up = sb("off_up", DH)
        mh = sb("mh", 64)
        id16 = sb("id16", HB, HB)
        before, after = sb("before", E, E), sb("after", E, E)

        cen, sq = sb("cen", NT, D), sb("sq", NT, D)
        st = sb("st", 3, NT)
        v_room = sb("v_room", 5 * TOK + 4)
        vf = v_room[:, 4 * TOK:5 * TOK + 4].rearrange("p (b l) -> p b l", b=2)
        vt = v_room[:, 0:TOK].rearrange("p (m c) -> p m c", c=C)
        sf = [v_room[:, TOK * k:TOK * k + TOK].rearrange("p (b l) -> p b l", b=2) for k in (1, 2, 3)]
        sft = sb("sft", M, C)
        qf, kf, tb = sb("qf", M, C), sb("kf", M, C), sb("tb", M, C)
        qk_hc, qk_sq = sb("qk_hc", 2, M, DH), sb("qk_sq", 2, M, DH)
        ss, rn = sb("ss", 2, M), sb("rn", 2, M)
        beta = sb("beta", M, C)
        kn_next = sb("kn_next", M, DH)
        kq_t = sb("kq_t", 2, M, C)
        kb = sb("kb", M, DH)
        nbm = sb("nbm", M, C)
        a_hc, a_t, a_off_t = sb("a_hc", M, C), sb("a_t", M, C), sb("a_off_t", M, C)
        attn_next = sb("attn_next", M, C)
        a_it, t_it, prod = sb("a_it", HB, HB), sb("t_it", HB, HB), sb("prod", HB * HB // 4)
        t16 = sb("t16", M, C)
        kn, q_t, attn_t = (taps_room[:, TOK * k:TOK * k + TOK].rearrange("p (m c) -> p m c", c=C) for k in range(3))
        vb = sb("vb", M, DH)
        t16_t, y_sb = sb("t16_t", M, C), sb("y_sb", M, C)
        t32_t, wneg_t = sb("t32_t", M, C), sb("wneg_t", M, C)
        u_sb, s_sb = sb("u_sb", 2, DH), sb("s_sb", 2, DH)
        paths = sb("paths", NP, M, DH)
        psq = sb("psq", NP, M, DH)
        pcen = toep_room[:, 0:NP * TOK].rearrange("p (a m d) -> p a m d", a=NP, m=M)
        pmean, pvar = sb("pmean", NP, M), sb("pvar", NP, M)
        stats, stats_t = sb("stats", M, C), sb("stats_t", M, C)
        hm = sb("hm", 2, TOK)
        lg = sb("lg", M, C)
        lb = sb("lb", M, NP)
        g0, g1, pr = sb("g0", M), sb("g1", M), sb("pr", M, NP)
        oh = sb("oh", M, DH)
        o_t = sb("o_t", TOK)
        x1 = sb("x1", NT, D)
        cen2, sq2 = cen, sq
        st2 = sb("st2", 4, NT)
        x2t = sb("x2t", TOK)
        rs, rt, ru = sb("rs", NT, E), sb("rt", NT, E), sb("ru", NT, E)
        cmp, cmq = sb("cmp", NT, E, E), sb("cmq", NT, E, E)
        sg = toep_room[:, NP * TOK:(NP + 2) * TOK].rearrange("p (k n) -> p k n", k=2)
        fu = v_room[:, 0:4 * TOK].rearrange("p (k f n) -> p k f n", k=2, f=FC)

        ps = [ctx.enter_context(nc.psum_tensor(f"ps{i}", [P, 512], F32)) for i in range(8)]
        A1_BANK, A2_BANK, GATE, VALUE, YB = (0, 1), (2, 3, 4), 5, 6, 7

        shear_d = nc.dram_tensor("shear_d", [C, D, LAGS * C], F32).ap()
        a_d = nc.dram_tensor("a_d", [M, P, C], F32).ap()
        t_d = nc.dram_tensor("t_d", [M, P, C], F32).ap()

        names = """early_loaded late_loaded expert_loaded x_first_loaded x_rest_loaded zeros_ready consts_ready pool_consts shear_stored
        toep_loaded t_zeroed w_scaled
        xn_ready xt_done xt_copied v_proj v_silu vt_ready v_copied short_ready sft_ready s_copied ln_sq ln_ms ln_rs
        fir_done long_ready temp_act temp_vec stats_zero
        q_done k_done beta_done q_silu k_silu b_tanh bt_ready qk_ready qk_squared ms_ready rn_ready beta_ready kq_ready
        kb_ready nbm_ready g_done a_ready attn_ready at_ready aoff_ready a_stored a_items t_items t_stored t16_loaded
        moved vb_ready t16t_ready y_done y_ready t32_done t32_ready w_done w_ready u_done s_done o_done
        p_copied delta_ready cen_ready psq_ready stats_ready hmid_done hm_ready lg_done ex_in ex_out mix_ready
        osq_ready om_ready orn_ready ot_ready wo_done x1_ready
        b_cen b_sq b_ms b_rs xn2_ready x2t_done x2t_ready r_done r_in r_ex gate_done val_done sg_ready fu_ready
        y2_done acc_done out_stored v_vec v_pool a1_vec a2_vec b_vec a1_pool""".split()
        s = {n: sem(n) for n in names}
        u_ready = [sem(f"u_ready{n}") for n in range(NC)]
        s_ready = [sem(f"s_ready{n}") for n in range(NC - 1)]

        def freed(eng, name, value):
            if not (isinstance(value, int) and value <= 0):
                eng.wait_ge(s[name], value)

        def chained(eng, name, t, total):
            count = [0]

            def link(ins, n=1):
                count[0] += n
                ins.then_inc(s[name], 1)
                eng.wait_ge(s[name], t * total + count[0])

            def end():
                assert count[0] == total, (name, count[0])

            link.end = end
            return link

        def pipeline(eng, body):
            body(1, 0, None)
            with eng.Fori(1, NPAIR - 1) as t:
                body(t + 1, t, t - 1)
            body(None, NPAIR - 1, NPAIR - 2)
            body(None, None, NPAIR - 1)

        def v_pipeline(eng, front, back):
            front(0)
            front(1)
            back(0)
            with eng.Fori(1, NPAIR - 1) as t:
                front(t + 1)
                back(t)
            back(NPAIR - 1)

        block = ctx.enter_context(nc.Block())
        x_d = x.rearrange("b (u p) d -> p (b u) d", p=P)
        out_d = out.rearrange("b (u p) d -> p (b u) d", p=P)

        @block.sync
        def _(sp):
            sp.dma_start(x_sb[:, 0:NT, :], x_d[:, 0:NT, :]).then_inc(s["x_first_loaded"], 16)
            sp.dma_start(early_sb[:, :], early).then_inc(s["early_loaded"], 16)
            sp.dma_start(taps_room[:, :], taps_row.partition_broadcast(P)).then_inc(s["early_loaded"], 16)
            for i in range(1, NPAIR):
                sp.dma_start(x_sb[:, NT * i:NT * i + NT, :], x_d[:, NT * i:NT * i + NT, :]).then_inc(s["x_rest_loaded"], 16)
            sp.wait_ge(s["zeros_ready"], 1)
            sp.dma_start(shear_d.rearrange("s (g c) k -> (s g) (c k)", g=4), toep_room[:, :]).then_inc(s["shear_stored"], 16)
            sp.dma_start(late_sb[:, :], late).then_inc(s["late_loaded"], 16)
            sp.wait_ge(s["shear_stored"], 16)
            sheared = bass.AP(shear_d.tensor, 0, [[D * LAGS * C + 1, C], [LAGS * C, D], [1, KL]])
            sp.dma_start(sheared, flr.partition_broadcast(C)).then_inc(s["shear_stored"], 16)
            sp.wait_ge(s["zeros_ready"], 2)
            sp.dma_start(t_d.rearrange("m p j -> p m j"), t16[:, :, :]).then_inc(s["t_zeroed"], 16)
            sp.wait_ge(s["shear_stored"], 32)
            for h in range(H):
                sp.dma_start(toep[C * h:C * h + C, :, :], shear_d[:, C * h:C * h + C, :]).then_inc(s["toep_loaded"], 16)
            for dst, src in ((w11_sb[:], w11.rearrange("e d f -> d e f")), (w12_sb[:], w12.rearrange("e d f -> d e f")),
                             (w2_sb[:], w2.rearrange("e (c p) d -> p (e c) d", p=P))):
                sp.dma_start(dst, src).then_inc(s["expert_loaded"], 16)
            sp.wait_ge(s["t_zeroed"], 16)

            def first(u):
                sp.wait_ge(s["a_ready"], u + 1)
                sp.dma_start(a_d.rearrange("m p j -> p m j"), a_hc[:, :, :]).then_inc(s["a_stored"], 16)
                sp.wait_ge(s["a_stored"], u * 16 + 16)
                blocks = a_d.rearrange("m (h k i) j -> k (m h) i j", h=H, k=2)
                for k in range(2):
                    sp.dma_start(a_it[64 * k:64 * k + 64, :, :],
                                 blocks[k, :, :, HB * k:HB * k + HB]).then_inc(s["a_items"], 16)
                sp.wait_ge(s["t_items"], u + 1)
                tblocks = t_d.rearrange("m (h k i) j -> k (m h) i j", h=H, k=2)
                for k in range(2):
                    sp.dma_start(tblocks[k, :, :, HB * k:HB * k + HB],
                                 t_it[64 * k:64 * k + 64, :, :]).then_inc(s["t_stored"], 16)
                freed(sp, "y_done", u)
                freed(sp, "t16t_ready", u)
                sp.wait_ge(s["t_stored"], u * 32 + 32)
                sp.dma_start(t16[:, :, :], t_d.rearrange("m p j -> p m j")).then_inc(s["t16_loaded"], 16)

            first(0)
            first(1)
            with sp.Fori(1, NPAIR - 1) as t:
                first(t + 1)

        @block.gpsimd
        def _(pool):
            count = [0]

            def link(ins):
                count[0] += 1
                ins.then_inc(s["pool_consts"], 1)
                pool.wait_ge(s["pool_consts"], count[0])

            link(pool.memset(ones[:], 1.0))
            pool.memset(toep_room[:], 0.0).then_inc(s["zeros_ready"], 1)
            link(pool.memset(mh[:], -0.5))
            for z in (xnp[:, :, 0:KS], v_hc[:, :, 0:2, :], vf[:, :, 0:2]):
                link(pool.memset(z, 0.0))
            link(pool.affine_select(out=ident[:], in_=ones[:], compare_op=ALU.is_equal, fill=0.0, base=0,
                                    pattern=[[-1, P]], channel_multiplier=1))
            PADS = count[0]

            def front(t):
                pool.wait_ge(s["ln_ms"], t + 1)
                pool.tensor_tensor(st[:, 2, :], st[:, 1, :], mh[:, 0:NT], ALU.pow).then_inc(s["ln_rs"], 1)

            def back(t):
                chain = chained(pool, "v_pool", t, V_POOL)
                pool.wait_ge(s["v_silu"], t + 1)
                freed(pool, "sft_ready", t)
                pool.tensor_tensor(sf[0], vf[:, :, 0:L], fs_sb[:, 0:1].unsqueeze(1).to_broadcast([P, 2, L]),
                                   ALU.mult).then_inc(s["v_pool"], 1)
                pool.tensor_scalar(sf[1], vf[:, :, 1:1 + L], fs_sb[:, 1:2], 1.0, ALU.mult, ALU.mult).then_inc(s["v_pool"], 1)
                chain(pool.tensor_scalar(sf[2], vf[:, :, 2:2 + L], fs_sb[:, 2:3], 1.0, ALU.mult, ALU.mult), 3)
                chain(pool.tensor_tensor(sf[1], sf[0], sf[1], ALU.add))
                pool.tensor_tensor(sf[2], sf[1], sf[2], ALU.add).then_inc(s["short_ready"], 1)
                chain.end()

            v_pipeline(pool, front, back)
            for z, v in ((t16, 0.0), (neg_low, -1.0), (keep_up, 1.0), (off_up, 1.0), (before, 1.0), (after, 1.0),
                         (id16, 1.0), (w2e, 0.0)):
                ins = pool.memset(z[:], v)
                if z is t16:
                    ins.then_inc(s["zeros_ready"], 1)
                else:
                    link(ins)
            for h in range(H):
                q = slice(C * h, C * h + C)
                link(pool.affine_select(out=neg_low[q, :], in_=neg_low[q, :], compare_op=ALU.is_gt, fill=0.0,
                                        base=0, pattern=[[-1, C]], channel_multiplier=1))
                link(pool.affine_select(out=keep_up[q, :], in_=keep_up[q, :], compare_op=ALU.is_ge, fill=0.0,
                                        base=0, pattern=[[1, C]], channel_multiplier=-1))
                link(pool.affine_select(out=off_up[q, :], in_=off_up[q, :], compare_op=ALU.is_ge, fill=0.0,
                                        base=HB - 1, pattern=[[0, C]], channel_multiplier=-1))
                link(pool.affine_select(out=off_up[q, :], in_=off_up[q, :], compare_op=ALU.is_ge, fill=0.0,
                                        base=-HB, pattern=[[1, C]], channel_multiplier=0))
            link(pool.affine_select(out=before[:], in_=before[:], compare_op=ALU.is_gt, fill=0.0, base=0,
                                    pattern=[[1, E], [-1, E]], channel_multiplier=0))
            link(pool.affine_select(out=after[:], in_=after[:], compare_op=ALU.is_gt, fill=0.0, base=0,
                                    pattern=[[-1, E], [1, E]], channel_multiplier=0))
            link(pool.affine_select(out=id16[:], in_=id16[:], compare_op=ALU.is_equal, fill=0.0, base=0,
                                    pattern=[[1, HB], [-1, HB]], channel_multiplier=0))
            pool.memset(stats[:], 0.0).then_inc(s["consts_ready"], 1)

            def first(u):
                chain = chained(pool, "a1_pool", u, A1_POOL)
                pool.wait_ge(s["beta_ready"], u + 1)
                pool.tensor_tensor(nbm[:, :, :], beta[:, :, :], neg_low[:, :].unsqueeze(1).to_broadcast([P, M, C]),
                                   ALU.mult).then_inc(s["nbm_ready"], 1)
                pool.wait_ge(s["ms_ready"], u + 1)
                pool.tensor_tensor(rn[:, :, :], ss[:, :, :], mh[:, 0:2 * M].rearrange("p (a m) -> p a m", a=2),
                                   ALU.pow).then_inc(s["rn_ready"], 1)
                pool.wait_ge(s["at_ready"], u + 1)
                freed(pool, "y_done", u)
                pool.tensor_tensor(a_off_t[:, :, :], a_t[:, :, :], off_up[:, :].unsqueeze(1).to_broadcast([P, M, C]),
                                   ALU.mult).then_inc(s["aoff_ready"], 1)
                pool.wait_ge(s["a_items"], u * 32 + 32)
                freed(pool, "t_stored", u * 32)
                chain(pool.tensor_tensor(t_it[:, :, :], a_it[:, :, :], id16[:, :, :], ALU.add))
                for j in range(1, HB - 1):
                    n = HB - 1 - j
                    pj = prod[:, 0:n * j].rearrange("p (i k) -> p i k", k=j)
                    chain(pool.tensor_tensor(pj, a_it[:, j + 1:HB, j:j + 1].to_broadcast([P, n, j]),
                                             t_it[:, j:j + 1, 0:j].to_broadcast([P, n, j]), ALU.mult))
                    ins = pool.tensor_tensor(t_it[:, j + 1:HB, 0:j], t_it[:, j + 1:HB, 0:j], pj, ALU.add)
                    if j < HB - 2:
                        chain(ins)
                    else:
                        ins.then_inc(s["t_items"], 1)
                chain.end()

            def body(u, t, b):
                if b is not None:
                    pool.wait_ge(s["b_ms"], b + 1)
                    pool.tensor_tensor(st2[:, 2, :], st2[:, 1, :], mh[:, 0:NT], ALU.pow).then_inc(s["b_rs"], 1)
                if u is not None:
                    first(u)
                if t is not None:
                    pool.wait_ge(s["om_ready"], t + 1)
                    pool.tensor_tensor(g1[:, :], g0[:, :], mh[:, 0:M], ALU.pow).then_inc(s["orn_ready"], 1)

            first(0)
            pipeline(pool, body)

        @block.tensor
        def _(pe):
            def heads(bank, col, n, lhs, rhs, **kw):
                for h in range(H):
                    q = slice(C * h, C * h + C)
                    ins = pe.matmul(bank[q, col:col + n], lhs(q), rhs(q), skip_group_check=True, **kw)
                return ins

            def chunks(ms, bank, n, lhs, rhs):
                for m in ms:
                    ins = heads(bank(m), n * m % 512, n, lambda q: lhs(q, m), lambda q: rhs(q, m),
                                start=True, stop=True)
                return ins

            def held():
                pe.wait_ge(s["pool_consts"], PADS_READY)

            def counts(*values):
                out = []
                for v in values:
                    if not isinstance(v, int):
                        v = pe.snap(v)
                        pe.wait_ge(s["toep_loaded"], v)
                    out.append(v)
                return out

            pe.wait_ge(s["pool_consts"], PADS_READY)

            def v_pass(t):
                pe.wait_ge(s["xn_ready"], t + 1)
                for j in range(NT):
                    ins = pe.transpose(ps[0][:, P * j:P * j + P], cen[:, j, :], ident[:, :])
                ins.then_inc(s["xt_done"], 1)
                pe.wait_ge(s["w_scaled"], 4)
                pe.wait_ge(s["xt_copied"], t + 1)
                for k in range(4):
                    ins = pe.matmul(ps[1][:, :], wvc[:, k, :], xnp[:, bass.ds(t * 2, 2), k:k + L],
                                    start=(k == 0), stop=(k == 3))
                ins.then_inc(s["v_proj"], 1)

            v_pass(0)
            with pe.Fori(1, NPAIR) as t:
                v_pass(t)

            def conv(bank, w, u, done):
                for k in range(4):
                    ins = pe.matmul(ps[bank][:, :], w[:, k, :], xnp[:, bass.ds(u * 2, 2), k:k + L],
                                    start=(k == 0), stop=(k == 3))
                ins.then_inc(s[done], 1)

            def project(u):
                pe.wait_ge(s["w_scaled"], 13)
                freed(pe, "attn_ready", u)
                conv(1, wkc, u, "k_done")
                conv(0, wqc, u, "q_done")

            def project_beta(u):
                pe.wait_ge(s["k_silu"], u + 1)
                pe.matmul(ps[1][:, :], wbe[:, :, :], xnp[:, bass.ds(u * 2, 2), KS:KS + L],
                          start=True, stop=True).then_inc(s["beta_done"], 1)

            def scores(u1, half):
                if half == 0:
                    held()
                    pe.wait_ge(s["kq_ready"], u1)
                    pe.wait_ge(s["q_silu"], u1)
                    pe.wait_ge(s["b_tanh"], u1)
                ins = chunks(range(8 * half, 8 * half + 8), lambda m: ps[m // 8], 64, lambda q, m: kq_t[q, 0, m, :],
                             lambda q, m: kq_t[q, :, m, :])
                ins.then_inc(s["g_done"], 1)

            def long_filter(quarter):
                for c in range(8 * quarter, 8 * quarter + 8):
                    for lag in range(LAGS):
                        ins = heads(ps[2 + quarter], c % 8 * B * NC, B * NC,
                                    lambda q: toep[q, c, C * lag:C * lag + C],
                                    lambda q: v_hc[q, :, 2 - lag:2 - lag + NC, c],
                                    start=(lag == 0), stop=(lag == LAGS - 1))
                ins.then_inc(s["fir_done"], 1)

            project(0)
            pe.wait_ge(s["v_copied"], NPAIR)
            pe.wait_ge(s["toep_loaded"], 64)
            long_filter(0)
            project_beta(0)
            long_filter(1)
            long_filter(2)
            scores(1, 0)
            scores(1, 1)
            long_filter(3)
            pe.wait_ge(s["long_ready"], 4)

            def body(u, t, b):
                (u1,) = counts(u + 1) if u is not None else (None,)
                (t1, t_16) = counts(t + 1, t * 16 + 16) if t is not None else (None, None)

                def gate_value(i):
                    if b is None:
                        return
                    e, f = i // FC, i % FC
                    if i:
                        pe.wait_ge(s["sg_ready"], b * E * FC + i)
                    else:
                        pe.wait_ge(s["x2t_ready"], b + 1)
                    pe.matmul(ps[GATE][:, :], w11_sb[:, e, P * f:P * f + P], x2t[:, :],
                              start=True, stop=True).then_inc(s["gate_done"], 1)
                    if i:
                        pe.wait_ge(s["fu_ready"], b * E * FC + i)
                    pe.matmul(ps[VALUE][:, :], w12_sb[:, e, P * f:P * f + P], x2t[:, :],
                              start=True, stop=True).then_inc(s["val_done"], 1)

                def down(e):
                    if b is None:
                        return
                    pe.wait_ge(s["fu_ready"], b * E * FC + FC * e + FC)
                    if e == 0:
                        pe.wait_ge(s["r_in"], b + 1)
                    else:
                        pe.wait_ge(s["acc_done"], b * E + e)
                    for j in range(NT):
                        for f in range(FC):
                            ins = pe.matmul(ps[YB][:, P * j:P * j + P], fu[:, e % 2, f, P * j:P * j + P],
                                            w2_sb[:, FC * e + f, :], start=(f == 0), stop=(f == FC - 1))
                    ins.then_inc(s["y2_done"], 1)

                def g_half(half):
                    if u is not None:
                        scores(u1, half)

                if u is not None:
                    project(u)
                if t is not None:
                    held()
                    freed(pe, "x1_ready", t)
                    pe.wait_ge(s["aoff_ready"], t1)
                    pe.wait_ge(s["t16_loaded"], t_16)
                    chunks(range(M), lambda m: ps[4], 32, lambda q, m: a_off_t[q, m, :],
                           lambda q, m: t16[q, m, :]).then_inc(s["y_done"], 1)
                if b is not None:
                    pe.wait_ge(s["xn2_ready"], b + 1)
                    for j in range(NT):
                        ins = pe.transpose(ps[YB][:, P * j:P * j + P], cen2[:, j, :], ident[:, :])
                    ins.then_inc(s["x2t_done"], 1)
                if u is not None:
                    project_beta(u)
                if t is not None:
                    held()
                    pe.wait_ge(s["y_ready"], t1)
                    pe.wait_ge(s["t16t_ready"], t1)
                    chunks(range(M), lambda m: ps[2], 32, lambda q, m: y_sb[q, m, :],
                           lambda q, m: t16_t[q, m, :]).then_inc(s["t32_done"], 1)
                if b is not None:
                    pe.wait_ge(s["expert_loaded"], 48)
                    pe.wait_ge(s["x2t_ready"], b + 1)
                    for j in range(NT):
                        ins = pe.matmul(ps[YB][:, E * j:E * j + E], x2t[:, P * j:P * j + P], wg_sb,
                                        start=True, stop=True)
                    ins.then_inc(s["r_done"], 1)
                if t is not None:
                    held()
                    pe.wait_ge(s["t32_ready"], t1)
                    pe.wait_ge(s["kb_ready"], t1)
                    chunks(range(M), lambda m: ps[3], 32, lambda q, m: kb[q, m, :],
                           lambda q, m: t32_t[q, m, :]).then_inc(s["w_done"], 1)

                def between(slot):
                    for what, i in SLOTS[slot]:
                        {"gv": gate_value, "y": down, "g": g_half}[what](i)

                for n in range(NC):
                    if t is not None:
                        held()
                        if n == 0:
                            pe.wait_ge(s["w_ready"], t1)
                            pe.wait_ge(s["vb_ready"], t1)
                            pe.wait_ge(s["moved"], t1)
                        else:
                            pe.wait_ge(s_ready[n - 1], t1)
                        for k in range(2):
                            m = k * NC + n
                            ins = heads(ps[4], DH * k, DH, lambda q: t32_t[q, m, :], lambda q: vb[q, m, :],
                                        start=True, stop=(n == 0))
                            if n:
                                ins = heads(ps[4], DH * k, DH, lambda q: wneg_t[q, m, :], lambda q: s_sb[q, k, :],
                                            start=False, stop=True)
                        ins.then_inc(s["u_done"], 1)
                    between(2 * n)
                    if t is not None:
                        held()
                        pe.wait_ge(u_ready[n], t1)
                        if n < NC - 1:
                            for k in range(2):
                                m = k * NC + n
                                ins = heads(ps[3], DH * k, DH, lambda q: kn[q, m, :], lambda q: u_sb[q, k, :],
                                            start=(n == 0 and k == 0), stop=(n == NC - 2))
                            ins.then_inc(s["s_done"], 1)
                        for k in range(2):
                            m = k * NC + n
                            if n:
                                heads(ps[2], DH * m, DH, lambda q: q_t[q, m, :], lambda q: s_sb[q, k, :],
                                      start=True, stop=False)
                            ins = heads(ps[2], DH * m, DH, lambda q: attn_t[q, m, :], lambda q: u_sb[q, k, :],
                                        start=(n == 0), stop=True)
                        ins.then_inc(s["o_done"], 1)
                    between(2 * n + 1)
                between(16)
                if t is not None:
                    pe.wait_ge(s["stats_ready"], t + 1)
                    for k in range(2):
                        pe.matmul(ps[2 + k][:, :], w1x[:, P * k:P * k + P], xnp[:, bass.ds(t * 2, 2), KS:KS + L],
                                  start=True, stop=False)
                        pe.matmul(ps[2 + k][:, :], w1s[:, P * k:P * k + P],
                                  stats_t[:, :, :].rearrange("p m t -> p (m t)"),
                                  start=False, stop=True).then_inc(s["hmid_done"], 1)
                between(17)
                if t is not None:
                    pe.wait_ge(s["hm_ready"], t * 2 + 2)
                    for k in range(2):
                        ins = pe.matmul(ps[4][:, :], w2e[:, k, :, :].rearrange("p h j -> p (h j)"), hm[:, k, :],
                                        start=(k == 0), stop=(k == 1))
                    ins.then_inc(s["lg_done"], 1)
                between(18)
                if t is not None:
                    pe.wait_ge(s["ot_ready"], t + 1)
                    for j in range(NT):
                        ins = pe.matmul(ps[2][:, P * j:P * j + P], o_t[:, P * j:P * j + P], wo_sb,
                                        start=True, stop=True)
                    ins.then_inc(s["wo_done"], 1)

            pipeline(pe, body)

        @block.scalar
        def _(act):
            half = "p (b l) -> p b l"

            def square(t):
                act.wait_ge(s["v_vec"], t * V_VEC + 2)
                act.activation(sq[:, :, :], cen[:, :, :], ACT.Square).then_inc(s["ln_sq"], 1)

            def xn_out(t):
                act.wait_ge(s["pool_consts"], PADS_READY)
                act.wait_ge(s["xt_done"], t + 1)
                act.activation(xnp[:, bass.ds(t * 2, 2), KS:KS + L], ps[0][:, :].rearrange(half, b=2),
                               ACT.Copy).then_inc(s["xt_copied"], 1)

            def back(t):
                act.wait_ge(s["v_proj"], t + 1)
                freed(act, "vt_ready", t)
                freed(act, "short_ready", t)
                act.activation(vf[:, :, 2:2 + L], ps[1][:, :].rearrange(half, b=2), ACT.Silu).then_inc(s["v_silu"], 1)
                act.wait_ge(s["vt_ready"], t + 1)
                act.activation(v_hc[:, bass.ds(t * 2, 2), 2:2 + NC, :].rearrange("p b n d -> p b (n d)"),
                               vt.rearrange("p (b n) d -> p b (n d)", b=2), ACT.Copy).then_inc(s["v_copied"], 1)
                act.wait_ge(s["sft_ready"], t + 1)
                act.activation(short_hc[:, bass.ds(t * M, M), :], sft[:, :, :], ACT.Copy).then_inc(s["s_copied"], 1)

            square(0)
            xn_out(0)
            square(1)
            back(0)
            with act.Fori(1, NPAIR - 1) as t:
                xn_out(t)
                square(t + 1)
                back(t)
            xn_out(NPAIR - 1)
            back(NPAIR - 1)

            bank = "p (m t) -> p m t"

            def project(u):
                act.wait_ge(s["k_done"], u + 1)
                act.activation(kf[:, :, :], ps[1][:, :].rearrange(bank, m=M), ACT.Silu).then_inc(s["k_silu"], 1)
                act.wait_ge(s["q_done"], u + 1)
                act.activation(qf[:, :, :], ps[0][:, :].rearrange(bank, m=M), ACT.Silu).then_inc(s["q_silu"], 1)
                act.wait_ge(s["qk_ready"], u * 2 + 2)
                act.activation(qk_sq[:, :, :, :], qk_hc[:, :, :, :], ACT.Square).then_inc(s["qk_squared"], 1)

            def project_beta(u):
                act.wait_ge(s["beta_done"], u + 1)
                act.activation(tb[:, :, :], ps[1][:, :].rearrange(bank, m=M), ACT.Tanh, scale=0.5).then_inc(s["b_tanh"], 1)

            project(0)
            project_beta(0)
            for c in range(4):
                act.wait_ge(s["fir_done"], c + 1)
                act.activation(long_hc[:, :, 8 * c:8 * c + 8].rearrange("p m c -> p c m"),
                               ps[2 + c][:, :].rearrange("p (c m) -> p c m", c=8), ACT.Copy).then_inc(s["long_ready"], 1)
            act.wait_ge(s["late_loaded"], 16)
            act.activation(temp[:, 1:2], logt, ACT.Abs).then_inc(s["temp_act"], 1)
            act.wait_ge(s["temp_act"], 1)
            act.activation(temp[:, 2:3], temp[:, 1:2], ACT.Exp, scale=-1.0).then_inc(s["temp_act"], 1)
            act.wait_ge(s["temp_act"], 2)
            act.activation(temp[:, 3:4], temp[:, 2:3], ACT.Ln, bias=1.0).then_inc(s["temp_act"], 1)
            act.activation(floor_hc, floor_hc, ACT.Sigmoid).then_inc(s["temp_act"], 1)
            act.wait_ge(s["v_copied"], NPAIR)
            act.wait_ge(s["s_copied"], NPAIR)
            act.wait_ge(s["long_ready"], 4)

            def body(u, t, b):
                def gate_value(i):
                    if b is None:
                        return
                    act.wait_ge(s["gate_done"], b * E * FC + i + 1)
                    if i >= 2:
                        act.wait_ge(s["fu_ready"], b * E * FC + i - 1)
                    act.activation(sg[:, i % 2, :], ps[GATE][:, :], ACT.Silu).then_inc(s["sg_ready"], 1)

                def between(slot):
                    for what, i in SLOTS[slot]:
                        if what == "gv":
                            gate_value(i)

                if t is not None:
                    freed(act, "x1_ready", t)
                    act.wait_ge(s["attn_ready"], t + 1)
                    act.activation(kn[:, :, :], kn_next[:, :, :], ACT.Copy)
                    act.activation(q_t[:, :, :], kq_t[:, 1, :, :], ACT.Copy)
                    act.activation(attn_t[:, :, :], attn_next[:, :, :], ACT.Copy).then_inc(s["moved"], 1)
                if b is not None:
                    act.wait_ge(s["b_cen"], b + 1)
                    act.activation(sq2[:, :, :], cen2[:, :, :], ACT.Square).then_inc(s["b_sq"], 1)
                if u is not None:
                    project(u)
                if t is not None:
                    act.wait_ge(s["y_done"], t + 1)
                    act.activation(y_sb[:, :, :], ps[4][:, :].rearrange(bank, m=M), ACT.Copy).then_inc(s["y_ready"], 1)
                if b is not None:
                    act.wait_ge(s["x2t_done"], b + 1)
                    act.activation(x2t[:, :], ps[YB][:, :], ACT.Copy).then_inc(s["x2t_ready"], 1)
                if u is not None:
                    project_beta(u)
                if b is not None:
                    act.wait_ge(s["r_in"], b + 1)
                    act.activation(rt[:, :, :], rs[:, :, :], ACT.Exp).then_inc(s["r_ex"], 1)
                if t is not None:
                    act.wait_ge(s["w_done"], t + 1)
                    act.activation(wneg_t[:, :, :], ps[3][:, :].rearrange(bank, m=M), ACT.Copy,
                                   scale=-1.0).then_inc(s["w_ready"], 1)
                for n in range(NC):
                    if t is not None:
                        act.wait_ge(s["u_done"], t * NC + n + 1)
                        if n:
                            act.wait_ge(s["o_done"], t * NC + n)
                        act.activation(u_sb[:, :, :], ps[4][:, 0:2 * DH].rearrange("p (b d) -> p b d", b=2),
                                       ACT.Copy).then_inc(u_ready[n], 1)
                    between(2 * n)
                    if t is not None and n < NC - 1:
                        act.wait_ge(s["s_done"], t * (NC - 1) + n + 1)
                        if n:
                            act.wait_ge(s["o_done"], t * NC + n + 1)
                        act.activation(s_sb[:, :, :], ps[3][:, 0:2 * DH].rearrange("p (b d) -> p b d", b=2),
                                       ACT.Copy).then_inc(s_ready[n], 1)
                    between(2 * n + 1)
                    if t is not None and n == 1:
                        for p, src in ((0, short_hc), (1, long_hc)):
                            act.activation(paths[:, p, :, :], src[:, bass.ds(t * M, M), :],
                                           ACT.Copy).then_inc(s["p_copied"], 1)
                        act.activation(paths[:, 3, :, :].rearrange("p (b n) d -> p b (n d)", b=2),
                                       v_hc[:, bass.ds(t * 2, 2), 2:2 + NC, :].rearrange("p b n d -> p b (n d)"),
                                       ACT.Copy).then_inc(s["p_copied"], 1)
                if t is not None:
                    act.wait_ge(s["o_done"], t * NC + NC)
                    act.activation(paths[:, 2, :, :], ps[2][:, :].rearrange("p (m d) -> p m d", m=M),
                                   ACT.Copy).then_inc(s["delta_ready"], 1)
                    act.wait_ge(s["cen_ready"], t + 1)
                    act.activation(psq[:, :, :, :], pcen[:, :, :, :], ACT.Square).then_inc(s["psq_ready"], 1)
                between(16)
                if t is not None:
                    for k in range(2):
                        act.wait_ge(s["hmid_done"], t * 2 + k + 1)
                        act.activation(hm[:, k, :], ps[2 + k][:, :], ACT.Gelu,
                                       bias=b1_sb[:, k:k + 1]).then_inc(s["hm_ready"], 1)
                between(17)
                if t is not None:
                    act.wait_ge(s["ex_in"], t + 1)
                    act.activation(pr[:, :, :], lb[:, :, :], ACT.Exp, scale=temp[:, 1:2]).then_inc(s["ex_out"], 1)
                between(18)
                if t is not None:
                    act.wait_ge(s["mix_ready"], t + 1)
                    act.activation(psq[:, 0, :, :], oh[:, :, :], ACT.Square).then_inc(s["osq_ready"], 1)
                if b is not None:
                    act.wait_ge(s["acc_done"], b * E + E)
                    act.dma_start(out_d[:, bass.ds(b * NT, NT), :], x1[:, :, :]).then_inc(s["out_stored"], 16)

            pipeline(act, body)
            act.wait_ge(s["out_stored"], 16 * NPAIR)

        @block.vector
        def _(dve):
            def flat(a):
                return a.rearrange("p m c -> p (m c)")

            def scaled(dst, src, k):
                for j in range(4):
                    dve.tensor_tensor(dst[:, j, :], src, taps[:, k, j, :], ALU.mult).then_inc(s["w_scaled"], 1)

            def front(t):
                chain = chained(dve, "v_vec", t, V_VEC)
                xt = x_sb[:, bass.ds(t * NT, NT), :]
                if isinstance(t, int):
                    dve.wait_ge(*((s["x_first_loaded"], 16) if t == 0 else (s["x_rest_loaded"], 48)))
                freed(dve, "xt_done", t)
                chain(dve.tensor_reduce(st[:, 0, :], xt, AX.X, ALU.add))
                chain(dve.scalar_tensor_tensor(cen[:, :, :], st[:, 0, :].unsqueeze(2).to_broadcast([P, NT, D]),
                                               -1.0 / D, xt, ALU.mult, ALU.add))
                if isinstance(t, int) and t == 0:
                    dve.wait_ge(s["early_loaded"], 32)
                    scaled(wvc, wv_sb, 2)
                dve.wait_ge(s["ln_sq"], t + 1)
                dve.tensor_reduce(st[:, 1, :], sq[:, :, :], AX.X, ALU.add).then_inc(s["temp_vec"], 1)
                dve.wait_ge(s["temp_vec"], t + 1)
                dve.tensor_scalar(st[:, 1, :], st[:, 1, :], 1.0 / D, 1e-5, ALU.mult, ALU.add).then_inc(s["ln_ms"], 1)
                dve.wait_ge(s["ln_rs"], t + 1)
                dve.tensor_tensor(cen[:, :, :], cen[:, :, :], st[:, 2, :].unsqueeze(2).to_broadcast([P, NT, D]),
                                  ALU.mult).then_inc(s["xn_ready"], 1)
                chain.end()

            def back(t):
                dve.wait_ge(s["v_silu"], t + 1)
                freed(dve, "v_copied", t)
                for b in range(2):
                    ins = dve.transpose(vt[:, NC * b:NC * b + NC, :].rearrange("p n c -> p (n c)"), vf[:, b, 2:2 + L])
                ins.then_inc(s["vt_ready"], 1)
                dve.wait_ge(s["short_ready"], t + 1)
                freed(dve, "s_copied", t)
                dve.transpose(flat(sft[:, :, :]), sf[2].rearrange("p b l -> p (b l)")).then_inc(s["sft_ready"], 1)

            v_pipeline(dve, front, back)

            dve.wait_ge(s["late_loaded"], 16)
            scaled(wkc, wk_sb, 1)
            scaled(wqc, wq_sb, 0)
            dve.tensor_copy(wbe[:, :, :], wb_sb.unsqueeze(2).to_broadcast([P, H, C])).then_inc(s["w_scaled"], 1)

            def to_hc(u, chain):
                dve.wait_ge(s["k_silu"], u + 1)
                dve.transpose(flat(qk_hc[:, 1, :, :]), flat(kf[:, :, :])).then_inc(s["qk_ready"], 1)
                dve.wait_ge(s["q_silu"], u + 1)
                dve.transpose(flat(qk_hc[:, 0, :, :]), flat(qf[:, :, :])).then_inc(s["qk_ready"], 1)
                dve.wait_ge(s["qk_squared"], u + 1)
                chain(dve.tensor_reduce(ss[:, :, :], qk_sq[:, :, :, :], AX.X, ALU.add))
                dve.tensor_scalar(ss[:, :, :], ss[:, :, :], 1e-6, None, ALU.add).then_inc(s["ms_ready"], 1)

            def to_beta(u, chain):
                dve.wait_ge(s["b_tanh"], u + 1)
                chain(dve.transpose(flat(beta[:, :, :]), flat(tb[:, :, :])))
                dve.tensor_scalar(beta[:, :, :], beta[:, :, :], 0.5, 0.5, ALU.mult, ALU.add).then_inc(s["beta_ready"], 1)

            def normalise(u, chain):
                dve.wait_ge(s["rn_ready"], u + 1)
                freed(dve, "moved", u)
                chain(dve.tensor_tensor(kn_next[:, :, :], qk_hc[:, 1, :, :],
                                        rn[:, 1, :].unsqueeze(2).to_broadcast([P, M, DH]), ALU.mult))
                dve.transpose(flat(kq_t[:, 0, :, :]), flat(kn_next[:, :, :]))
                chain(dve.tensor_tensor(qk_hc[:, 0, :, :], qk_hc[:, 0, :, :],
                                        rn[:, 0, :].unsqueeze(2).to_broadcast([P, M, DH]), ALU.mult))
                dve.transpose(flat(kq_t[:, 1, :, :]), flat(qk_hc[:, 0, :, :])).then_inc(s["kq_ready"], 1)
                dve.wait_ge(s["beta_ready"], u + 1)
                freed(dve, "w_done", u)
                dve.tensor_tensor(kb[:, :, :], kn_next[:, :, :], beta[:, :, :], ALU.mult).then_inc(s["kb_ready"], 1)

            def masks(u, chain):
                dve.wait_ge(s["nbm_ready"], u + 1)
                for k in range(2):
                    dve.wait_ge(s["g_done"], u * 2 + k + 1)
                    g = ps[k][:, :].rearrange("p (m a j) -> p m a j", m=8, a=2)
                    ins = dve.tensor_tensor(a_hc[:, 8 * k:8 * k + 8, :], g[:, :, 0, :], nbm[:, 8 * k:8 * k + 8, :],
                                            ALU.mult)
                    if k == 0:
                        chain(ins)
                    else:
                        ins.then_inc(s["a_ready"], 1)
                dve.wait_ge(s["a_ready"], u + 1)
                dve.transpose(flat(a_t[:, :, :]), flat(a_hc[:, :, :])).then_inc(s["at_ready"], 1)
                for k in range(2):
                    g = ps[k][:, :].rearrange("p (m a j) -> p m a j", m=8, a=2)
                    ins = dve.tensor_tensor(attn_next[:, 8 * k:8 * k + 8, :], g[:, :, 1, :],
                                            keep_up[:, :].unsqueeze(1).to_broadcast([P, 8, C]), ALU.mult)
                    if k == 0:
                        chain(ins)
                    else:
                        ins.then_inc(s["attn_ready"], 1)
                chain.end()

            first = chained(dve, "a1_vec", 0, A1_VEC)
            to_hc(0, first)
            to_beta(0, first)
            normalise(0, first)
            dve.wait_ge(s["pool_consts"], ALL_CONSTS)
            dve.wait_ge(s["consts_ready"], 1)
            masks(0, first)

            dve.wait_ge(s["temp_act"], 4)
            step = chained(dve, "stats_zero", 0, 6)
            step(dve.tensor_scalar(temp[:, 0:1], logt, 0.0, None, ALU.max))
            step(dve.tensor_tensor(temp[:, 0:1], temp[:, 0:1], temp[:, 3:4], ALU.add))
            step(dve.tensor_scalar(temp[:, 0:1], temp[:, 0:1], 1e-4, None, ALU.add))
            step(dve.reciprocal(temp[:, 1:2], temp[:, 0:1]))
            step(dve.tensor_scalar(floor_hc, floor_hc, 0.05, None, ALU.mult))
            step(dve.tensor_copy(w2e[:, :, :, 0:NP], w2r.rearrange("p (k h j) -> p k h j", k=2, h=H)))
            step.end()
            dve.wait_ge(s["long_ready"], 4)

            def body(u, t, b):
                if u is not None:
                    first = chained(dve, "a1_vec", u, A1_VEC)
                if t is not None:
                    chain = chained(dve, "a2_vec", t, A2_VEC)
                if b is not None:
                    chain_b = chained(dve, "b_vec", b, B_VEC)

                def weigh():
                    dve.wait_ge(s["r_ex"], b + 1)
                    chain_b(dve.tensor_reduce(st2[:, 3, :], rt[:, :, :], AX.X, ALU.add))
                    chain_b(dve.reciprocal(st2[:, 3, :], st2[:, 3, :]))
                    chain_b(dve.tensor_tensor(rt[:, :, :], rt[:, :, :], st2[:, 3, :].unsqueeze(2).to_broadcast([P, NT, E]),
                                              ALU.mult))
                    for j in range(NT):
                        of = rt[:, j:j + 1, :].to_broadcast([P, E, E])
                        oe = rt[:, j, :].unsqueeze(2).to_broadcast([P, E, E])
                        dve.tensor_tensor(cmp[:, j, :, :], of, oe, ALU.is_ge)
                        ins = dve.tensor_tensor(cmq[:, j, :, :], of, oe, ALU.is_gt)
                    chain_b(ins)
                    fl = "p j e f -> p j (e f)"
                    bc = [P, NT, E * E]
                    chain_b(dve.tensor_tensor(cmp[:, :, :, :].rearrange(fl), cmp[:, :, :, :].rearrange(fl),
                                              before[:, :, :].rearrange("p e f -> p (e f)").unsqueeze(1).to_broadcast(bc),
                                              ALU.mult))
                    chain_b(dve.tensor_tensor(cmq[:, :, :, :].rearrange(fl), cmq[:, :, :, :].rearrange(fl),
                                              after[:, :, :].rearrange("p e f -> p (e f)").unsqueeze(1).to_broadcast(bc),
                                              ALU.mult))
                    chain_b(dve.tensor_tensor(cmp[:], cmp[:], cmq[:], ALU.add))
                    chain_b(dve.tensor_reduce(ru[:, :, :], cmp[:, :, :, :], AX.X, ALU.add))
                    chain_b(dve.scalar_tensor_tensor(rs[:, :, :], ru[:, :, :], 1.5, rt[:, :, :], ALU.is_lt, ALU.mult))
                    chain_b(dve.tensor_reduce(st2[:, 3, :], rs[:, :, :], AX.X, ALU.add))
                    chain_b(dve.tensor_scalar(st2[:, 3, :], st2[:, 3, :], 1e-8, None, ALU.add))
                    chain_b(dve.reciprocal(st2[:, 3, :], st2[:, 3, :]))
                    chain_b(dve.tensor_tensor(rs[:, :, :], rs[:, :, :], st2[:, 3, :].unsqueeze(2).to_broadcast([P, NT, E]),
                                              ALU.mult))
                    chain_b.end()

                def gate_value(i):
                    if b is None:
                        return
                    e, f = i // FC, i % FC
                    dve.wait_ge(s["sg_ready"], b * E * FC + i + 1)
                    dve.wait_ge(s["val_done"], b * E * FC + i + 1)
                    if e >= 2:
                        dve.wait_ge(s["y2_done"], b * E + e - 1)
                    dve.tensor_tensor(fu[:, e % 2, f, :], sg[:, i % 2, :], ps[VALUE][:, :],
                                      ALU.mult).then_inc(s["fu_ready"], 1)

                def down(e):
                    if b is None:
                        return
                    dve.wait_ge(s["y2_done"], b * E + e + 1)
                    if e >= 1:
                        dve.wait_ge(s["acc_done"], b * E + e)
                    for j in range(NT):
                        ins = dve.scalar_tensor_tensor(x1[:, j, :], ps[YB][:, P * j:P * j + P], rs[:, j, e:e + 1],
                                                       x1[:, j, :], ALU.mult, ALU.add)
                    ins.then_inc(s["acc_done"], 1)

                def masked(half):
                    if u is not None and half == 1:
                        masks(u, first)

                def between(slot):
                    for what, i in SLOTS[slot]:
                        {"gv": gate_value, "y": down, "g": masked}[what](i)

                if t is not None:
                    dve.wait_ge(s["t16_loaded"], t * 16 + 16)
                    dve.transpose(flat(t16_t[:, :, :]), flat(t16[:, :, :])).then_inc(s["t16t_ready"], 1)
                if b is not None:
                    dve.wait_ge(s["x1_ready"], b + 1)
                    chain_b(dve.tensor_reduce(st2[:, 0, :], x1[:, :, :], AX.X, ALU.add))
                    dve.scalar_tensor_tensor(cen2[:, :, :], st2[:, 0, :].unsqueeze(2).to_broadcast([P, NT, D]), -1.0 / D,
                                             x1[:, :, :], ALU.mult, ALU.add).then_inc(s["b_cen"], 1)
                if t is not None:
                    dve.tensor_tensor(vb[:, :, :].rearrange("p (b n) d -> p b (n d)", b=2),
                                      v_hc[:, bass.ds(t * 2, 2), 2:2 + NC, :].rearrange("p b n d -> p b (n d)"),
                                      beta[:, :, :].rearrange("p (b n) d -> p b (n d)", b=2),
                                      ALU.mult).then_inc(s["vb_ready"], 1)
                if b is not None:
                    dve.wait_ge(s["b_sq"], b + 1)
                    chain_b(dve.tensor_reduce(st2[:, 1, :], sq2[:, :, :], AX.X, ALU.add))
                    dve.tensor_scalar(st2[:, 1, :], st2[:, 1, :], 1.0 / D, 1e-5, ALU.mult, ALU.add).then_inc(s["b_ms"], 1)
                    dve.wait_ge(s["b_rs"], b + 1)
                    dve.tensor_tensor(cen2[:, :, :], cen2[:, :, :], st2[:, 2, :].unsqueeze(2).to_broadcast([P, NT, D]),
                                      ALU.mult).then_inc(s["xn2_ready"], 1)
                if u is not None:
                    to_hc(u, first)
                if t is not None:
                    dve.wait_ge(s["t16t_ready"], t + 1)
                    dve.wait_ge(s["t32_done"], t + 1)
                    dve.tensor_tensor(t32_t[:, :, :], ps[2][:, :].rearrange("p (m t) -> p m t", m=M), t16_t[:, :, :],
                                      ALU.add).then_inc(s["t32_ready"], 1)
                if u is not None:
                    to_beta(u, first)
                if b is not None:
                    dve.wait_ge(s["r_done"], b + 1)
                    chain_b(dve.tensor_reduce(st2[:, 3, :], ps[YB][:, 0:NT * E].rearrange("p (j e) -> p j e", e=E), AX.X,
                                              ALU.max))
                    dve.tensor_tensor(rs[:, :, :], ps[YB][:, 0:NT * E].rearrange("p (j e) -> p j e", e=E),
                                      st2[:, 3, :].unsqueeze(2).to_broadcast([P, NT, E]), ALU.subtract).then_inc(s["r_in"], 1)
                if u is not None:
                    normalise(u, first)
                if b is not None:
                    weigh()
                for slot in range(16):
                    between(slot)
                if t is not None:
                    dve.wait_ge(s["p_copied"], t * 3 + 3)
                    dve.wait_ge(s["delta_ready"], t + 1)
                    chain(dve.tensor_reduce(pmean[:, :, :], paths[:, :, :, :], AX.X, ALU.add))
                    chain(dve.tensor_scalar(pmean[:, :, :], pmean[:, :, :], 1.0 / DH, None, ALU.mult))
                    fp = "p a m d -> p (a m) d"
                    dve.tensor_tensor(pcen[:, :, :, :].rearrange(fp), paths[:, :, :, :].rearrange(fp),
                                      pmean[:, :, :].rearrange("p a m -> p (a m)").unsqueeze(2).to_broadcast([P, NP * M, DH]),
                                      ALU.subtract).then_inc(s["cen_ready"], 1)
                    dve.tensor_copy(stats[:, :, 0:8:2].rearrange("p m a -> p a m"), pmean[:, :, :])
                    dve.wait_ge(s["psq_ready"], t + 1)
                    chain(dve.tensor_reduce(pvar[:, :, :], psq[:, :, :, :], AX.X, ALU.add))
                    chain(dve.tensor_scalar(stats[:, :, 1:8:2].rearrange("p m a -> p a m"), pvar[:, :, :], 1.0 / DH, None,
                                            ALU.mult))
                    dve.transpose(flat(stats_t[:, :, :]), flat(stats[:, :, :])).then_inc(s["stats_ready"], 1)
                between(16)
                between(17)
                if t is not None:
                    dve.wait_ge(s["lg_done"], t + 1)
                    chain(dve.transpose(flat(lg[:, :, :]), ps[4][:, :]))
                    chain(dve.tensor_tensor(lb[:, :, :], lg[:, :, 0:NP], bias_hc.unsqueeze(1).to_broadcast([P, M, NP]),
                                            ALU.add))
                    chain(dve.tensor_reduce(g0[:, :], lb[:, :, :], AX.X, ALU.max))
                    dve.tensor_tensor(lb[:, :, :], lb[:, :, :], g0[:, :].unsqueeze(2).to_broadcast([P, M, NP]),
                                      ALU.subtract).then_inc(s["ex_in"], 1)
                    dve.wait_ge(s["ex_out"], t + 1)
                    for again in range(2):
                        chain(dve.tensor_reduce(g0[:, :], pr[:, :, :], AX.X, ALU.add))
                        chain(dve.reciprocal(g0[:, :], g0[:, :]))
                        chain(dve.tensor_tensor(pr[:, :, :], pr[:, :, :], g0[:, :].unsqueeze(2).to_broadcast([P, M, NP]),
                                                ALU.mult))
                        if not again:
                            chain(dve.tensor_tensor(pr[:, :, :], pr[:, :, :],
                                                    floor_hc.unsqueeze(1).to_broadcast([P, M, NP]), ALU.max))
                    for p in range(NP):
                        ins = dve.tensor_tensor(pcen[:, p, :, :], paths[:, p, :, :],
                                                pr[:, :, p:p + 1].to_broadcast([P, M, DH]), ALU.mult)
                    chain(ins)
                    chain(dve.tensor_tensor(pcen[:, 0:2, :, :], pcen[:, 0:2, :, :], pcen[:, 2:4, :, :], ALU.add))
                    dve.tensor_tensor(oh[:, :, :], pcen[:, 0, :, :], pcen[:, 1, :, :], ALU.add).then_inc(s["mix_ready"], 1)
                between(18)
                if t is not None:
                    dve.wait_ge(s["osq_ready"], t + 1)
                    chain(dve.tensor_reduce(g0[:, :], psq[:, 0, :, :], AX.X, ALU.add))
                    dve.tensor_scalar(g0[:, :], g0[:, :], 1.0 / DH, 1e-5, ALU.mult, ALU.add).then_inc(s["om_ready"], 1)
                    dve.wait_ge(s["orn_ready"], t + 1)
                    chain(dve.tensor_tensor(oh[:, :, :], oh[:, :, :], g1[:, :].unsqueeze(2).to_broadcast([P, M, DH]),
                                            ALU.mult))
                    dve.tensor_tensor(oh[:, :, :], oh[:, :, :], on_sb.unsqueeze(1).to_broadcast([P, M, DH]),
                                      ALU.mult).then_inc(s["bt_ready"], 1)
                    dve.wait_ge(s["bt_ready"], t + 1)
                    dve.transpose(o_t[:, :], flat(oh[:, :, :])).then_inc(s["ot_ready"], 1)
                    dve.wait_ge(s["wo_done"], t + 1)
                    freed(dve, "out_stored", t * 16)
                    dve.tensor_tensor(x1[:, :, :], ps[2][:, :].rearrange("p (j d) -> p j d", j=NT),
                                      x_sb[:, bass.ds(t * NT, NT), :], ALU.add).then_inc(s["x1_ready"], 1)
                    chain.end()

            pipeline(dve, body)


_OUT = (B, L, D)


def kernel(**inputs):
    import numpy as np
    import concourse.bacc as bacc
    from concourse.bass_utils import run_bass_kernel_spmd

    a = {k.split("_", 2)[2]: np.asarray(v) for k, v in inputs.items()}

    def heads(v):
        return np.repeat(v.reshape(H, -1), C, axis=0)

    w1 = a["gate_w1"].T
    w1s = np.pad(w1[D:].reshape(NP, H, 2, HID).transpose(1, 0, 2, 3).reshape(H, 2 * NP, HID),
                 ((0, 0), (0, C - 2 * NP), (0, 0))).reshape(P, HID)
    early = np.concatenate([a["Wv"].T, a["Wb"].T, a["fir_short_w"].reshape(D, KS)], axis=1)
    late = np.concatenate([a["Wq"].T, a["Wk"].T, a["Wo"].T, w1[:D], w1s, a["gate_b1"].reshape(2, P).T,
                           a["gate_w2"].T.reshape(2, P, H * NP).transpose(1, 0, 2).reshape(P, 2 * H * NP), a["Wg"],
                           heads(a["base_bias"]), heads(a["floor_raw"]), heads(a["log_temp"]),
                           np.repeat(a["onorm_w"].reshape(1, DH), P, axis=0)], axis=1)
    taps = np.concatenate([a[n].T.reshape(-1) for n in ("qconv_w", "kconv_w", "vconv_w")])
    laid = [("x", a["hidden_states"]), ("early", early), ("taps", taps), ("late", late),
            ("flr", a["fir_long_w"].reshape(D, KL)[:, ::-1]), ("w11", a["W11"]), ("w12", a["W12"]), ("w2", a["W2"])]
    nc = bacc.Bacc("TRN2", target_bir_lowering=False, num_devices=1)
    arrays, args = {}, []
    for name, v in laid:
        v = np.ascontiguousarray(v)
        arrays[f"in_{name}"] = v
        args.append(nc.dram_tensor(f"in_{name}", v.shape, mybir.dt.from_np(v.dtype), kind="ExternalInput").ap())
    args.append(nc.dram_tensor("out_y", _OUT, F32, kind="ExternalOutput").ap())
    build(nc, *args)
    r = run_bass_kernel_spmd(nc, [arrays], core_ids=[0])
    return r.results[0]["out_y"]
```

```python
from contextlib import ExitStack

import concourse.bass as bass
from concourse import mybir

F32 = mybir.dt.float32
F32R = mybir.dt.float32r
ALU = mybir.AluOpType
ACT = mybir.ActivationFunctionType
AX = mybir.AxisListType

P = 128
B, L, D = 8, 256, 128
H, DH = 4, 32
C = 32
NPAIR = B // 2
TOK = 2 * L
NT = TOK // P
M = TOK // C
NC = L // C
HB = C // 2
KS, KL = 3, 63
LAGS = 3
NP = 4
HID = 256
E, FF = 8, 256
FC = FF // P

A1_VEC, A2_VEC, MIX_VEC, A1_POOL, B_VEC = 6, 22, 5, 28, 16

PADS_READY, ALL_CONSTS = 7, 33

def gv(*halves):
    return [(what, i) for i in halves for what in ("gate", "sig", "value", "fuse")]


def y(e):
    return [("y", e), ("add", e)]


def centre(p):
    return [("centre", p), ("square", p)]


START = [("conv", 0), ("t16t", 0), ("mix0", 1), ("mix1", 1), ("mix2", 1), ("t16", 0), ("conv", 1), ("conv", 2),
         ("vb", 0), ("y_out", 0), ("k_silu", 0), ("k_hc", 0), ("mix_sq", 1), ("t32", 0), ("conv", 3), ("moved", 0),
         ("scale0", 1), ("t32_add", 0), ("scale1", 1), ("w", 0), ("w_out", 0), ("out", 1), ("ln_cen", 1),
         ("ln_sq", 1)]
SCAN = [[("ln_var", 1)], [("ln_out", 1)], [("x2t", 1)], [("q_silu", 0), ("q_hc", 0), ("qk_sq", 0), ("norms", 0)],
        [("router", 1), ("beta", 0), ("tanh", 0), ("beta_hc", 0)],
        [("gate", 0), ("sig", 0), ("value", 0), ("fuse", 0)],
        [("gate", 1), ("sig", 1), ("value", 1), ("fuse", 1), ("norm", 0), ("gate", 2)],
        [("sig", 2), ("value", 2), ("gate", 3), ("fuse", 2)], [("g", 0), ("weigh", 0)], [("g", 1), ("mask", 0)],
        [("sig", 3), ("value", 3), ("fuse", 3), ("centre", 0), ("square", 0)],
        [("y", 0), ("add", 0), ("centre", 3), ("spread", 0)], [("gate", 4), ("sig", 4), ("value", 4), ("fuse", 4)],
        [("gate", 5), ("square", 3), ("sig", 5), ("value", 5), ("spread", 3)], [("fuse", 5)],
        [("gate", 6), ("y", 1), ("add", 1), ("sig", 6), ("value", 6), ("centre", 1), ("square", 1)]]
TAIL = [("fuse", 6), ("delta", 0), ("gate", 7), ("sig", 7), ("value", 7), ("centre", 2), ("spread", 1), ("fuse", 7),
        ("y", 2), ("add", 2), ("gate", 8), ("sig", 8), ("value", 8), ("fuse", 8), ("square", 2), ("spread", 2),
        ("gate", 9), ("sig", 9), ("value", 9), ("fuse", 9), ("stats", 0), ("hidden_x", 0), ("y", 3), ("gate", 10),
        ("sig", 10), ("add", 3), ("value", 10), ("fuse", 10), ("hidden_s", 0), ("y", 4), ("add", 4), ("gelu", 0),
        ("gate", 11), ("sig", 11), ("value", 11), ("fuse", 11), ("gate", 12), ("sig", 12), ("value", 12),
        ("fuse", 12), ("y", 5), ("add", 5), ("logits", 0), ("gate", 13), ("sig", 13), ("value", 13), ("fuse", 13),
        ("exp_in", 0), ("gate", 14), ("sig", 14), ("value", 14), ("fuse", 14), ("y", 6), ("add", 6), ("exp", 0),
        ("gate", 15), ("sig", 15), ("value", 15), ("fuse", 15), ("softmax", 0), ("y", 7), ("add", 7)]
rest = [("fir", channel) for channel in range(DH // 2, DH)]
for what, count in (("t16", 2), ("t32", 2), ("w", 2)):
    at = START.index((what, 0)) + 1
    START[at:at] = rest[:count]
    del rest[:count]
for items in SCAN[:-1]:
    if rest and not any(what == "g" for what, _ in items):
        items.append(rest.pop(0))
assert not rest
SCAN[6].append(("split", 0))
SCAN[9].append(("reload", 0))
SCAN[12].append(("split", 1))
after = TAIL.index(("softmax", 0)) + 1
LAST_TAIL = TAIL[:after] + [("mix0", 0), ("mix1", 0), ("mix2", 0), ("mix_sq", 0), ("scale0", 0)]
LAST_TAIL += TAIL[after:] + [("scale1", 0)]
ALONE = [item for item in [("out", 1), ("ln_cen", 1), ("ln_sq", 1), ("ln_var", 1), ("ln_out", 1), ("x2t", 1),
                           ("router", 1)] if item not in START] + [("weigh", 0), *gv(0, 1, 2, 3)]
for expert in range(E):
    ALONE += [*y(expert), *gv(*(i for i in (2 * expert + 4, 2 * expert + 5) if i < E * FC))]
PATHS = (0, 3, 1, 2)


def build(nc, x, early, taps_row, late, flr, w11, w12, w2, out):
    ctx = ExitStack()
    with ctx:
        def sb(name, *shape):
            return ctx.enter_context(nc.sbuf_tensor(name, [P, *shape], F32))

        def sem(name):
            return ctx.enter_context(nc.semaphore(name))

        def parts(room, *widths):
            at = 0
            for w in widths:
                yield room[:, at:at + w]
                at += w

        x_sb = sb("x_sb", 2 * B, D)
        xnp = sb("xnp", B, KS + L)
        v_hc = sb("v_hc", B, 2 + NC, DH)
        short_hc = sb("short_hc", B * NC, DH)
        long_hc = sb("long_hc", B * NC, DH)
        toep_room = sb("toep_room", DH * LAGS * C)
        toep = toep_room[:, :].rearrange("p (c k) -> p c k", c=DH)
        early_sb = sb("early_sb", D + H + KS)
        wv_sb, wb_sb, fs_sb = parts(early_sb, D, H, KS)
        late_sb = sb("late_sb", 3 * D + 2 * HID + 2 + 2 * H * NP + E + 2 * NP + 2)
        (wq_sb, wk_sb, wo_sb, w1x, w1s, b1_sb, w2r, wg_sb, bias_hc, floor_hc, logt, on_sb) = parts(
            late_sb, D, D, D, HID, HID, 2, 2 * H * NP, E, NP, NP, 1, 1)
        taps_room = sb("taps_room", 3 * 4 * D)
        taps = taps_room[:, :].rearrange("p (k j d) -> p k j d", k=3, j=4)
        wqc, wkc, wvc = sb("wqc", 4, D), sb("wkc", 4, D), sb("wvc", 4, D)
        wbe = sb("wbe", H, C)
        w2e = sb("w2e", 2, H, C)
        w11_sb, w12_sb = sb("w11_sb", E, FF), sb("w12_sb", E, FF)
        w11_lo, w12_lo = sb("w11_lo", E, FF), sb("w12_lo", E, FF)
        w2_sb = sb("w2_sb", E * FC, D)
        temp = sb("temp", 4)
        ones, ident = sb("ones", P), sb("ident", P)
        neg_low = sb("neg_low", DH)
        keep_up = sb("keep_up", DH)
        off_up = sb("off_up", DH)
        mh = sb("mh", 64)
        id16 = sb("id16", HB, HB)
        before, after = sb("before", E, E), sb("after", E, E)

        st = sb("st", 3, 2 * B)
        v_room = sb("v_room", 4 * TOK + 8)
        vf = [v_room[:, (TOK + 4) * k:(TOK + 4) * (k + 1)].rearrange("p (b l) -> p b l", b=2) for k in range(2)]
        sf = [v_room[:, TOK * k + 8:TOK * k + TOK + 8].rearrange("p (b l) -> p b l", b=2) for k in (2, 3)]
        qf, kf, tb = sb("qf", M, C), sb("kf", M, C), sb("tb", M, C)
        qk_hc, qk_sq = sb("qk_hc", 2, M, DH), sb("qk_sq", 2, M, DH)
        ss, rn = sb("ss", 2, M), sb("rn", 2, M)
        beta = sb("beta", M, C)
        kn_next = sb("kn_next", M, DH)
        kq_t = sb("kq_t", 2, M, C)
        kb = sb("kb", M, DH)
        nbm = sb("nbm", M, C)
        a_hc, a_t, a_off_t = sb("a_hc", M, C), sb("a_t", M, C), sb("a_off_t", M, C)
        attn_next = sb("attn_next", M, C)
        a_it, t_it, prod = sb("a_it", HB, HB), sb("t_it", HB, HB), sb("prod", HB * HB // 4)
        t16 = sb("t16", M, C)
        kn, q_t, attn_t = (taps_room[:, TOK * k:TOK * k + TOK].rearrange("p (m c) -> p m c", c=C) for k in range(3))
        vb = sb("vb", M, DH)
        t16_t, y_sb = sb("t16_t", M, C), sb("y_sb", M, C)
        t32_t, wneg_t = sb("t32_t", M, C), sb("wneg_t", M, C)
        u_sb, s_sb = sb("u_sb", 2, DH), sb("s_sb", 2, DH)
        delta_hc = sb("delta_hc", M, DH)
        psq = sb("psq", NP, M, DH)
        pcen = toep_room[:, 0:NP * TOK].rearrange("p (a m d) -> p a m d", a=NP, m=M)
        xn = psq[:, :, :, :].rearrange("p a m d -> p (a m d)").rearrange("p (j d) -> p j d", d=D)
        xsq = w2_sb
        pmean, pvar = sb("pmean", NP, M), sb("pvar", NP, M)
        stats, stats_t = sb("stats", M, C), sb("stats_t", M, C)
        hm = sb("hm", 2, TOK)
        lg = sb("lg", M, C)
        lb = sb("lb", M, NP)
        g0, gm, g1, pr = sb("g0", M), sb("gm", M), sb("g1", M), sb("pr", M, NP)
        oh = sb("oh", M, DH)
        o_t = sb("o_t", TOK)
        x1 = sb("x1", NT, D)
        cen2 = sb("cen2", NT, D)
        sq2 = psq[:, NP - 1, :, :].rearrange("p m d -> p (m d)").rearrange("p (j d) -> p j d", d=D)
        st2 = sb("st2", 4, NT)
        x2t, x2_hi, x2_lo = sb("x2t", TOK), sb("x2_hi", TOK), sb("x2_lo", TOK)
        rs, rt, ru = sb("rs", NT, E), sb("rt", NT, E), sb("ru", NT, E)
        cmp, cmq = (lg[:, M // 2 * k:M // 2 * k + M // 2, :].rearrange("p m t -> p (m t)").rearrange(
            "p (j e f) -> p j e f", e=E, f=E) for k in range(2))
        sg = toep_room[:, NP * TOK:(NP + 2) * TOK].rearrange("p (k n) -> p k n", k=2)
        raw = v_room[:, 0:E * FF].rearrange("p (e f) -> p e f", e=E)
        fu = v_room[:, 0:4 * TOK].rearrange("p (k f n) -> p k f n", k=2, f=FC)

        ps = [ctx.enter_context(nc.psum_tensor(f"ps{i}", [P, 512], F32)) for i in range(8)]
        GATE, VALUE, YB = (5, 0), (6, 1), 7

        FIR = (2, 3, 5, 6)

        shear_d = nc.dram_tensor("shear_d", [C, D, LAGS * C], F32).ap()
        a_d = nc.dram_tensor("a_d", [M, P, C], F32).ap()
        t_d = nc.dram_tensor("t_d", [M, P, C], F32).ap()

        names = """early_loaded late_loaded expert_loaded x_first_loaded x_rest_loaded zeros_ready consts_ready pool_consts shear_stored
        toep_loaded t_zeroed w_scaled
        xn_ready xt_done xt_copied v_proj v_silu v_ready short_first short_ready ln_cen ln_sq ln_ms ln_rs
        fir_done long_ready temp_act temp_vec stats_zero
        q_done k_done beta_done q_silu k_silu b_tanh bt_ready qk_ready qk_squared ms_ready rn_ready beta_ready kq_ready
        kb_ready nbm_ready g_done a_ready attn_ready at_ready aoff_ready a_stored a_items t_items t_stored t16_loaded
        moved vb_ready t16t_ready y_done y_ready t32_done t32_ready w_done w_ready u_done s_done o_done
        p_copied delta_ready cen_ready psq_ready stats_ready hmid_done hm_ready lg_done ex_in ex_out mix_ready
        osq_ready om_ready orn_ready mix_vec ot_ready wo_done x1_ready
        b_cen b_sq b_ms b_rs xn2_ready x2t_done x2t_ready x2_split w_split raw_loaded r_done r_in r_ex gate_done val_done sg_ready fu_ready
        y2_done acc_done out_stored v_vec a1_vec a2_vec b_vec a1_pool""".split()
        s = {n: sem(n) for n in names}
        u_ready = [sem(f"u_ready{n}") for n in range(NC)]
        s_ready = [sem(f"s_ready{n}") for n in range(NC - 1)]

        def freed(eng, name, value):
            if not (isinstance(value, int) and value <= 0):
                eng.wait_ge(s[name], value)

        def chained(eng, name, t, total):
            count = [0]

            def link(ins, n=1):
                count[0] += n
                ins.then_inc(s[name], 1)
                eng.wait_ge(s[name], t * total + count[0])

            def end():
                assert count[0] == total, (name, count[0])

            link.end = end
            return link

        def pipeline(eng, body):
            body(1, 0, None)
            with eng.Fori(1, NPAIR - 1) as t:
                body(t + 1, t, t - 1)
            body(None, NPAIR - 1, NPAIR - 2)
            body(None, None, NPAIR - 1)

        block = ctx.enter_context(nc.Block())
        x_d = x.rearrange("b (u p) d -> p (b u) d", p=P)
        out_d = out.rearrange("b (u p) d -> p (b u) d", p=P)

        def mixed(t, b, last):
            return t if not last else None if t is None else b

        PARTS = (slice(0, NT), slice(NT, 2 * B))

        @block.sync
        def _(sp):
            sp.dma_start(x_sb[:, 0:NT, :], x_d[:, 0:NT, :]).then_inc(s["x_first_loaded"], 16)
            sp.dma_start(early_sb[:, :], early).then_inc(s["early_loaded"], 16)
            sp.dma_start(taps_room[:, :], taps_row.partition_broadcast(P)).then_inc(s["early_loaded"], 16)
            sp.dma_start(late_sb[:, :], late).then_inc(s["late_loaded"], 16)
            sp.dma_start(x_sb[:, NT:2 * B, :], x_d[:, NT:2 * B, :]).then_inc(s["x_rest_loaded"], 16)
            sp.wait_ge(s["zeros_ready"], 1)
            sp.dma_start(shear_d.rearrange("s (g c) k -> (s g) (c k)", g=4), toep_room[:, :]).then_inc(s["shear_stored"], 16)
            sp.wait_ge(s["shear_stored"], 16)
            sheared = bass.AP(shear_d.tensor, 0, [[D * LAGS * C + 1, C], [LAGS * C, D], [1, KL]])
            sp.dma_start(sheared, flr.partition_broadcast(C)).then_inc(s["shear_stored"], 16)
            sp.wait_ge(s["zeros_ready"], 2)
            sp.dma_start(t_d.rearrange("m p j -> p m j"), t16[:, :, :]).then_inc(s["t_zeroed"], 16)
            sp.wait_ge(s["shear_stored"], 32)
            for h in range(H):
                sp.dma_start(toep[C * h:C * h + C, :, :], shear_d[:, C * h:C * h + C, :]).then_inc(s["toep_loaded"], 16)
            sp.wait_ge(s["ln_ms"], 2)
            sp.dma_start(w2_sb[:], w2.rearrange("e (c p) d -> p (e c) d", p=P)).then_inc(s["expert_loaded"], 16)
            sp.wait_ge(s["t_zeroed"], 16)

            def first(u):
                sp.wait_ge(s["a_ready"], u + 1)
                sp.dma_start(a_d.rearrange("m p j -> p m j"), a_hc[:, :, :]).then_inc(s["a_stored"], 16)
                sp.wait_ge(s["a_stored"], u * 16 + 16)
                blocks = a_d.rearrange("m (h k i) j -> k (m h) i j", h=H, k=2)
                for k in range(2):
                    sp.dma_start(a_it[64 * k:64 * k + 64, :, :],
                                 blocks[k, :, :, HB * k:HB * k + HB]).then_inc(s["a_items"], 16)
                sp.wait_ge(s["t_items"], u + 1)
                tblocks = t_d.rearrange("m (h k i) j -> k (m h) i j", h=H, k=2)
                for k in range(2):
                    sp.dma_start(tblocks[k, :, :, HB * k:HB * k + HB],
                                 t_it[64 * k:64 * k + 64, :, :]).then_inc(s["t_stored"], 16)
                freed(sp, "y_done", u)
                freed(sp, "t16t_ready", u)
                sp.wait_ge(s["t_stored"], u * 32 + 32)
                sp.dma_start(t16[:, :, :], t_d.rearrange("m p j -> p m j")).then_inc(s["t16_loaded"], 16)

            first(0)
            sp.wait_ge(s["v_ready"], NPAIR)
            sp.wait_ge(s["short_ready"], NPAIR)
            sp.dma_start(raw, w11.rearrange("e d f -> d e f")).then_inc(s["raw_loaded"], 16)
            first(1)
            with sp.Fori(1, NPAIR - 1) as t:
                first(t + 1)

        @block.gpsimd
        def _(pool):
            count = [0]

            def link(ins):
                count[0] += 1
                ins.then_inc(s["pool_consts"], 1)
                pool.wait_ge(s["pool_consts"], count[0])

            link(pool.memset(ones[:], 1.0))
            pool.memset(toep_room[:], 0.0).then_inc(s["zeros_ready"], 1)
            link(pool.memset(mh[:], -0.5))
            for z in (xnp[:, :, 0:KS], v_hc[:, :, 0:2, :], vf[0][:, :, 0:2], vf[1][:, :, 0:2]):
                link(pool.memset(z, 0.0))
            link(pool.affine_select(out=ident[:], in_=ones[:], compare_op=ALU.is_equal, fill=0.0, base=0,
                                    pattern=[[-1, P]], channel_multiplier=1))
            pool.memset(t16[:], 0.0).then_inc(s["zeros_ready"], 1)

            for g in range(2):
                pool.wait_ge(s["ln_ms"], g + 1)
                part = PARTS[g]
                pool.tensor_tensor(st[:, 2, part], st[:, 1, part], mh[:, part], ALU.pow).then_inc(s["ln_rs"], 1)

            for z, v in ((neg_low, -1.0), (keep_up, 1.0), (off_up, 1.0), (before, 1.0), (after, 1.0), (id16, 1.0),
                         (w2e, 0.0)):
                link(pool.memset(z[:], v))
            for h in range(H):
                q = slice(C * h, C * h + C)
                link(pool.affine_select(out=neg_low[q, :], in_=neg_low[q, :], compare_op=ALU.is_gt, fill=0.0,
                                        base=0, pattern=[[-1, C]], channel_multiplier=1))
                link(pool.affine_select(out=keep_up[q, :], in_=keep_up[q, :], compare_op=ALU.is_ge, fill=0.0,
                                        base=0, pattern=[[1, C]], channel_multiplier=-1))
                link(pool.affine_select(out=off_up[q, :], in_=off_up[q, :], compare_op=ALU.is_ge, fill=0.0,
                                        base=HB - 1, pattern=[[0, C]], channel_multiplier=-1))
                link(pool.affine_select(out=off_up[q, :], in_=off_up[q, :], compare_op=ALU.is_ge, fill=0.0,
                                        base=-HB, pattern=[[1, C]], channel_multiplier=0))
            link(pool.affine_select(out=before[:], in_=before[:], compare_op=ALU.is_gt, fill=0.0, base=0,
                                    pattern=[[1, E], [-1, E]], channel_multiplier=0))
            link(pool.affine_select(out=after[:], in_=after[:], compare_op=ALU.is_gt, fill=0.0, base=0,
                                    pattern=[[-1, E], [1, E]], channel_multiplier=0))
            link(pool.affine_select(out=id16[:], in_=id16[:], compare_op=ALU.is_equal, fill=0.0, base=0,
                                    pattern=[[1, HB], [-1, HB]], channel_multiplier=0))
            pool.memset(stats[:], 0.0).then_inc(s["consts_ready"], 1)

            def norms(u):
                pool.wait_ge(s["ms_ready"], u + 1)
                pool.tensor_tensor(rn[:, :, :], ss[:, :, :], mh[:, 0:2 * M].rearrange("p (a m) -> p a m", a=2),
                                   ALU.pow).then_inc(s["rn_ready"], 1)

            def first(u):
                chain = chained(pool, "a1_pool", u, A1_POOL)
                pool.wait_ge(s["beta_ready"], u + 1)
                pool.tensor_tensor(nbm[:, :, :], beta[:, :, :], neg_low[:, :].unsqueeze(1).to_broadcast([P, M, C]),
                                   ALU.mult).then_inc(s["nbm_ready"], 1)
                pool.wait_ge(s["at_ready"], u + 1)
                freed(pool, "y_done", u)
                pool.tensor_tensor(a_off_t[:, :, :], a_t[:, :, :], off_up[:, :].unsqueeze(1).to_broadcast([P, M, C]),
                                   ALU.mult).then_inc(s["aoff_ready"], 1)
                pool.wait_ge(s["a_items"], u * 32 + 32)
                freed(pool, "t_stored", u * 32)
                chain(pool.tensor_tensor(t_it[:, :, :], a_it[:, :, :], id16[:, :, :], ALU.add))
                for j in range(1, HB - 1):
                    n = HB - 1 - j
                    pj = prod[:, 0:n * j].rearrange("p (i k) -> p i k", k=j)
                    chain(pool.tensor_tensor(pj, a_it[:, j + 1:HB, j:j + 1].to_broadcast([P, n, j]),
                                             t_it[:, j:j + 1, 0:j].to_broadcast([P, n, j]), ALU.mult))
                    ins = pool.tensor_tensor(t_it[:, j + 1:HB, 0:j], t_it[:, j + 1:HB, 0:j], pj, ALU.add)
                    if j < HB - 2:
                        chain(ins)
                    else:
                        ins.then_inc(s["t_items"], 1)
                chain.end()

            def mix_norm(t):
                pool.wait_ge(s["om_ready"], t + 1)
                pool.tensor_tensor(g1[:, :], gm[:, :], mh[:, 0:M], ALU.pow).then_inc(s["orn_ready"], 1)

            def body(u, t, b):
                if b is not None and t is not None:
                    mix_norm(b)
                if b is not None:
                    pool.wait_ge(s["b_ms"], b + 1)
                    pool.tensor_tensor(st2[:, 2, :], st2[:, 1, :], mh[:, 0:NT], ALU.pow).then_inc(s["b_rs"], 1)
                if u is not None:
                    norms(u)
                    first(u)

                if u is None and t is not None:
                    mix_norm(t)

            norms(0)
            first(0)
            pipeline(pool, body)

        def two_banks(u, i):
            return u is None or i >= 4

        def bank_of(u, i):
            return i % 2 if two_banks(u, i) else 0

        def banks_before(u, i):
            return max((j for j in range(i) if bank_of(u, j) == bank_of(u, i)), default=None)

        def out_bank(t, e):
            return (YB, 2)[e % 2] if t is None else YB

        @block.tensor
        def _(pe):
            def heads(bank, col, n, lhs, rhs, **kw):
                for h in range(H):
                    q = slice(C * h, C * h + C)
                    ins = pe.matmul(bank[q, col:col + n], lhs(q), rhs(q), skip_group_check=True, **kw)
                return ins

            def chunks(ms, bank, n, lhs, rhs):
                for m in ms:
                    ins = heads(bank(m), n * m % 512, n, lambda q: lhs(q, m), lambda q: rhs(q, m),
                                start=True, stop=True)
                return ins

            def held():
                pe.wait_ge(s["pool_consts"], PADS_READY)

            def counts(*values):
                out = []
                for v in values:
                    if not isinstance(v, int):
                        v = pe.snap(v)
                        pe.wait_ge(s["toep_loaded"], v)
                    out.append(v)
                return out

            pe.wait_ge(s["pool_consts"], PADS_READY)

            def turn(i):
                pe.wait_ge(s["xn_ready"], min(i, 1) + 1)
                for j in range(NT):
                    ins = pe.transpose(ps[i][:, P * j:P * j + P], xn[:, NT * i + j, :], ident[:, :])
                ins.then_inc(s["xt_done"], 1)

            def project_v(i):
                pe.wait_ge(s["w_scaled"], 13)
                pe.wait_ge(s["xt_copied"], i + 1)
                for k in range(4):
                    ins = pe.matmul(ps[4 + i][:, :], wvc[:, k, :], xnp[:, 2 * i:2 * i + 2, k:k + L],
                                    start=(k == 0), stop=(k == 3))
                ins.then_inc(s["v_proj"], 1)

            def conv(u, part):
                if part == 0:
                    pe.wait_ge(s["w_scaled"], 8)
                    freed(pe, "attn_ready", u)
                bank, w, done = ((1, wkc, "k_done"), (0, wqc, "q_done"))[part // 2]
                for k in (part % 2 * 2, part % 2 * 2 + 1):
                    ins = pe.matmul(ps[bank][:, :], w[:, k, :], xnp[:, bass.ds(u * 2, 2), k:k + L],
                                    start=(k == 0), stop=(k == 3))
                if part % 2:
                    ins.then_inc(s[done], 1)

            def project(u):
                for part in range(4):
                    conv(u, part)

            def project_beta(u):
                pe.wait_ge(s["w_scaled"], 9)
                pe.wait_ge(s["k_silu"], u + 1)
                pe.matmul(ps[1][:, :], wbe[:, :, :], xnp[:, bass.ds(u * 2, 2), KS:KS + L],
                          start=True, stop=True).then_inc(s["beta_done"], 1)

            def scores(u1, half):
                if half == 0:
                    held()
                    pe.wait_ge(s["kq_ready"], u1)
                    pe.wait_ge(s["q_silu"], u1)
                    pe.wait_ge(s["b_tanh"], u1)
                ins = chunks(range(8 * half, 8 * half + 8), lambda m: ps[m // 8], 64, lambda q, m: kq_t[q, 0, m, :],
                             lambda q, m: kq_t[q, :, m, :])
                ins.then_inc(s["g_done"], 1)

            def long_filter(c):
                for lag in range(LAGS):
                    ins = heads(ps[FIR[c // 8]], c % 8 * B * NC, B * NC,
                                lambda q: toep[q, c, C * lag:C * lag + C],
                                lambda q: v_hc[q, :, 2 - lag:2 - lag + NC, c],
                                start=(lag == 0), stop=(lag == LAGS - 1))
                if c % 8 == 7:
                    ins.then_inc(s["fir_done"], 1)

            turn(0)
            pe.wait_ge(s["xt_copied"], 1)
            project(0)
            project_v(0)
            project_beta(0)
            pe.wait_ge(s["b_tanh"], 1)
            for i in range(1, NPAIR):
                turn(i)
            project_v(1)
            project_v(2)
            scores(1, 0)
            scores(1, 1)
            project_v(3)
            pe.wait_ge(s["v_ready"], NPAIR)
            pe.wait_ge(s["toep_loaded"], 64)
            for c in range(16):
                long_filter(c)
            project(1)
            pe.wait_ge(s["long_ready"], 2)

            def expert_product(bank, high, low, i):
                cols = (slice(None), i // FC, slice(P * (i % FC), P * (i % FC) + P))
                for k, (a, c) in enumerate(((high, x2_hi), (low, x2_hi), (high, x2_lo))):
                    ins = pe.matmul(bank[:, :], a[cols].bitcast(F32R), c[:, :].bitcast(F32R), start=(k == 0), stop=(k == 2))
                return ins

            def body(u, t, b):
                (u1,) = counts(u + 1) if u is not None else (None,)
                (t1, t_16) = counts(t + 1, t * 16 + 16) if t is not None else (None, None)

                def gate(i):
                    if b is None:
                        return
                    last = banks_before(u, i)
                    if i == 0:
                        pe.wait_ge(s["w_split"], 4)
                        pe.wait_ge(s["x2_split"], b * 2 + 2)
                    elif two_banks(u, i) and not two_banks(u, i - 1):
                        pe.wait_ge(s["attn_ready"], u + 1)
                    if last is not None:
                        pe.wait_ge(s["sg_ready"], b * E * FC + last + 1)
                    expert_product(ps[GATE[bank_of(u, i)]], w11_sb, w11_lo, i).then_inc(s["gate_done"], 1)

                def value(i):
                    if b is None:
                        return
                    last = banks_before(u, i)
                    if last is not None:
                        pe.wait_ge(s["fu_ready"], b * E * FC + last + 1)
                    expert_product(ps[VALUE[bank_of(u, i)]], w12_sb, w12_lo, i).then_inc(s["val_done"], 1)

                def down(e):
                    if b is None:
                        return
                    pe.wait_ge(s["fu_ready"], b * E * FC + FC * e + FC)
                    yb = ps[out_bank(t, e)]
                    if e == 0:
                        pe.wait_ge(s["r_in"], b + 1)
                    elif t is not None or e >= 2:
                        pe.wait_ge(s["acc_done"], b * E + e - (t is None))
                    for j in range(NT):
                        for f in range(FC):
                            ins = pe.matmul(yb[:, P * j:P * j + P], fu[:, e % 2, f, P * j:P * j + P],
                                            w2_sb[:, FC * e + f, :], start=(f == 0), stop=(f == FC - 1))
                    ins.then_inc(s["y2_done"], 1)

                def g_half(half):
                    if u is not None:
                        scores(u1, half)

                def fir(c):
                    if b is None:
                        long_filter(c)

                def hidden_x(_):
                    if t is not None:
                        pe.wait_ge(s["delta_ready"], t + 1)
                        for k in range(2):
                            pe.matmul(ps[2 + k][:, :], w1x[:, P * k:P * k + P], xnp[:, bass.ds(t * 2, 2), KS:KS + L],
                                      start=True, stop=False)

                def hidden_s(_):
                    if t is not None:
                        pe.wait_ge(s["stats_ready"], t + 1)
                        for k in range(2):
                            pe.matmul(ps[2 + k][:, :], w1s[:, P * k:P * k + P],
                                      stats_t[:, :, :].rearrange("p m t -> p (m t)"),
                                      start=False, stop=True).then_inc(s["hmid_done"], 1)

                def logits(_):
                    if t is not None:
                        pe.wait_ge(s["hm_ready"], t * 2 + 2)
                        for k in range(2):
                            ins = pe.matmul(ps[4][:, :], w2e[:, k, :, :].rearrange("p h j -> p (h j)"), hm[:, k, :],
                                            start=(k == 0), stop=(k == 1))
                        ins.then_inc(s["lg_done"], 1)

                def output(_):
                    if b is not None:
                        pe.wait_ge(s["ot_ready"], b + 1)
                        for j in range(NT):
                            ins = pe.matmul(ps[YB][:, P * j:P * j + P], o_t[:, P * j:P * j + P], wo_sb,
                                            start=True, stop=True)
                        ins.then_inc(s["wo_done"], 1)

                def project_qk(part):
                    if b is not None and u is not None:
                        conv(u, part)

                def beta_out(_):
                    if u is not None:
                        project_beta(u)

                def t16_off(_):
                    if t is not None:
                        held()
                        freed(pe, "ex_in", t)
                        pe.wait_ge(s["aoff_ready"], t1)
                        pe.wait_ge(s["t16_loaded"], t_16)
                        chunks(range(M), lambda m: ps[4], 32, lambda q, m: a_off_t[q, m, :],
                               lambda q, m: t16[q, m, :]).then_inc(s["y_done"], 1)

                def t32(_):
                    if t is not None:
                        held()
                        pe.wait_ge(s["y_ready"], t1)
                        pe.wait_ge(s["t16t_ready"], t1)
                        chunks(range(M), lambda m: ps[2], 32, lambda q, m: y_sb[q, m, :],
                               lambda q, m: t16_t[q, m, :]).then_inc(s["t32_done"], 1)

                def w(_):
                    if t is not None:
                        held()
                        pe.wait_ge(s["t32_ready"], t1)
                        pe.wait_ge(s["kb_ready"], t1)
                        chunks(range(M), lambda m: ps[3], 32, lambda q, m: kb[q, m, :],
                               lambda q, m: t32_t[q, m, :]).then_inc(s["w_done"], 1)

                def x2t_turn(_):
                    if b is not None:
                        pe.wait_ge(s["xn2_ready"], b + 1)
                        for j in range(NT):
                            ins = pe.transpose(ps[YB][:, P * j:P * j + P], cen2[:, j, :], ident[:, :])
                        ins.then_inc(s["x2t_done"], 1)

                def router(_):
                    if b is not None:
                        pe.wait_ge(s["expert_loaded"], 16)
                        pe.wait_ge(s["x2t_ready"], b + 1)
                        for j in range(NT):
                            ins = pe.matmul(ps[YB][:, E * j:E * j + E], x2t[:, P * j:P * j + P], wg_sb,
                                            start=True, stop=True)
                        ins.then_inc(s["r_done"], 1)

                steps = {"gate": gate, "value": value, "y": down, "g": g_half, "fir": fir, "hidden_x": hidden_x,
                         "hidden_s": hidden_s, "logits": logits, "out": output, "conv": project_qk, "beta": beta_out,
                         "t16": t16_off, "t32": t32, "w": w, "x2t": x2t_turn, "router": router}

                def run(items):
                    for what, i in items:
                        if what in steps:
                            steps[what](i)

                run(START)
                if t is None:
                    return run(ALONE)

                for n in range(NC):
                    if t is not None:
                        held()
                        if n == 0:
                            pe.wait_ge(s["w_ready"], t1)
                            pe.wait_ge(s["vb_ready"], t1)
                            pe.wait_ge(s["moved"], t1)
                        else:
                            pe.wait_ge(s_ready[n - 1], t1)
                        for k in range(2):
                            m = k * NC + n
                            ins = heads(ps[4], DH * k, DH, lambda q: t32_t[q, m, :], lambda q: vb[q, m, :],
                                        start=True, stop=(n == 0))
                            if n:
                                ins = heads(ps[4], DH * k, DH, lambda q: wneg_t[q, m, :], lambda q: s_sb[q, k, :],
                                            start=False, stop=True)
                        ins.then_inc(s["u_done"], 1)
                    run(SCAN[2 * n])
                    if t is not None:
                        held()
                        pe.wait_ge(u_ready[n], t1)
                        if n < NC - 1:
                            for k in range(2):
                                m = k * NC + n
                                ins = heads(ps[3], DH * k, DH, lambda q: kn[q, m, :], lambda q: u_sb[q, k, :],
                                            start=(n == 0 and k == 0), stop=(n == NC - 2))
                            ins.then_inc(s["s_done"], 1)
                        for k in range(2):
                            m = k * NC + n
                            if n:
                                heads(ps[2], DH * m, DH, lambda q: q_t[q, m, :], lambda q: s_sb[q, k, :],
                                      start=True, stop=False)
                            ins = heads(ps[2], DH * m, DH, lambda q: attn_t[q, m, :], lambda q: u_sb[q, k, :],
                                        start=(n == 0), stop=True)
                        ins.then_inc(s["o_done"], 1)
                    run(SCAN[2 * n + 1])
                run(TAIL if u is not None else LAST_TAIL)

            pipeline(pe, body)

        @block.scalar
        def _(act):
            half = "p (b l) -> p b l"

            def turn(i):
                act.wait_ge(s["xt_done"], i + 1)
                act.activation(xnp[:, 2 * i:2 * i + 2, KS:KS + L], ps[i][:, :].rearrange(half, b=2),
                               ACT.Copy).then_inc(s["xt_copied"], 1)

            act.wait_ge(s["pool_consts"], PADS_READY)
            for g in range(2):
                act.wait_ge(s["ln_cen"], g + 1)
                act.activation(xsq[:, PARTS[g], :], xn[:, PARTS[g], :], ACT.Square).then_inc(s["ln_sq"], 1)
                if g == 0:
                    turn(0)
            def project_v(i):
                act.wait_ge(s["v_proj"], i + 1)
                if i >= 2:
                    act.wait_ge(s["v_ready"], i - 1)
                    act.wait_ge(s["short_ready"], i - 1)
                act.activation(vf[i % 2][:, :, 2:2 + L], ps[4 + i][:, :].rearrange(half, b=2),
                               ACT.Silu).then_inc(s["v_silu"], 1)
                act.wait_ge(s["v_silu"], i + 1)
                act.activation(sf[i % 2], vf[i % 2][:, :, 0:L], ACT.Copy,
                               scale=fs_sb[:, 0:1]).then_inc(s["short_first"], 1)

            bank = "p (m t) -> p m t"

            def k_silu(u):
                act.wait_ge(s["k_done"], u + 1)
                act.activation(kf[:, :, :], ps[1][:, :].rearrange(bank, m=M), ACT.Silu).then_inc(s["k_silu"], 1)

            def q_silu(u):
                act.wait_ge(s["q_done"], u + 1)
                act.activation(qf[:, :, :], ps[0][:, :].rearrange(bank, m=M), ACT.Silu).then_inc(s["q_silu"], 1)

            def qk_squares(u):
                act.wait_ge(s["qk_ready"], u * 2 + 2)
                act.activation(qk_sq[:, :, :, :], qk_hc[:, :, :, :], ACT.Square).then_inc(s["qk_squared"], 1)

            def project(u):
                k_silu(u)
                q_silu(u)
                qk_squares(u)

            def project_beta(u):
                act.wait_ge(s["beta_done"], u + 1)
                act.activation(tb[:, :, :], ps[1][:, :].rearrange(bank, m=M), ACT.Tanh, scale=0.5).then_inc(s["b_tanh"], 1)

            project(0)
            project_v(0)
            project_beta(0)
            for i in range(1, NPAIR):
                turn(i)
            for i in range(1, NPAIR):
                project_v(i)
            act.wait_ge(s["late_loaded"], 16)
            act.activation(temp[:, 1:2], logt, ACT.Abs).then_inc(s["temp_act"], 1)
            act.wait_ge(s["temp_act"], 1)
            act.activation(temp[:, 2:3], temp[:, 1:2], ACT.Exp, scale=-1.0).then_inc(s["temp_act"], 1)
            act.wait_ge(s["temp_act"], 2)
            act.activation(temp[:, 3:4], temp[:, 2:3], ACT.Ln, bias=1.0).then_inc(s["temp_act"], 1)
            act.activation(floor_hc, floor_hc, ACT.Sigmoid).then_inc(s["temp_act"], 1)

            def long_out(c):
                act.wait_ge(s["fir_done"], c + 1)
                act.activation(long_hc[:, :, 8 * c:8 * c + 8].rearrange("p m c -> p c m"),
                               ps[FIR[c]][:, :].rearrange("p (c m) -> p c m", c=8), ACT.Copy).then_inc(s["long_ready"], 1)

            for c in range(2):
                long_out(c)
            project(1)

            def body(u, t, b):
                def gate(i):
                    if b is None:
                        return
                    act.wait_ge(s["gate_done"], b * E * FC + i + 1)
                    if i >= 2:
                        act.wait_ge(s["fu_ready"], b * E * FC + i - 1)
                    act.activation(sg[:, i % 2, :], ps[GATE[bank_of(u, i)]][:, :], ACT.Silu).then_inc(s["sg_ready"], 1)

                def reload(_):
                    if b is None:
                        act.wait_ge(s["w_split"], 2)
                        act.dma_start(raw, w12.rearrange("e d f -> d e f")).then_inc(s["raw_loaded"], 16)

                def fir(c):
                    if b is None and c % 8 == 7:
                        long_out(c // 8)

                def delta(_):
                    if t is not None:
                        act.wait_ge(s["o_done"], t * NC + NC)
                        act.activation(delta_hc[:, :, :], ps[2][:, :].rearrange("p (m d) -> p m d", m=M),
                                       ACT.Copy).then_inc(s["delta_ready"], 1)

                def square(p):
                    if t is not None:
                        act.wait_ge(s["cen_ready"], t * NP + PATHS.index(p) + 1)
                        act.activation(psq[:, p, :, :], pcen[:, p, :, :], ACT.Square).then_inc(s["psq_ready"], 1)

                def hidden(_):
                    if t is not None:
                        for k in range(2):
                            act.wait_ge(s["hmid_done"], t * 2 + k + 1)
                            act.activation(hm[:, k, :], ps[2 + k][:, :], ACT.Gelu,
                                           bias=b1_sb[:, k:k + 1]).then_inc(s["hm_ready"], 1)

                def exp_in(_):
                    if t is not None:
                        act.wait_ge(s["ex_in"], t + 1)
                        act.activation(pr[:, :, :], lb[:, :, :], ACT.Exp, scale=temp[:, 1:2]).then_inc(s["ex_out"], 1)

                def mix_sq(last):
                    pair = mixed(t, b, last)
                    if pair is not None:
                        act.wait_ge(s["mix_ready"], pair + 1)
                        act.activation(psq[:, 0, :, :], oh[:, :, :], ACT.Square).then_inc(s["osq_ready"], 1)

                def moved(_):
                    if t is not None:
                        act.wait_ge(s["attn_ready"], t + 1)
                        act.activation(kn[:, :, :], kn_next[:, :, :], ACT.Copy)
                        act.activation(q_t[:, :, :], kq_t[:, 1, :, :], ACT.Copy)
                        act.activation(attn_t[:, :, :], attn_next[:, :, :], ACT.Copy).then_inc(s["moved"], 1)

                def beside(step):
                    return lambda _: step(u) if b is not None and u is not None else None

                def tanh(_):
                    if u is not None:
                        project_beta(u)

                def y_out(_):
                    if t is not None:
                        act.wait_ge(s["y_done"], t + 1)
                        act.activation(y_sb[:, :, :], ps[4][:, :].rearrange(bank, m=M), ACT.Copy).then_inc(s["y_ready"], 1)

                def w_out(_):
                    if t is not None:
                        act.wait_ge(s["w_done"], t + 1)
                        act.activation(wneg_t[:, :, :], ps[3][:, :].rearrange(bank, m=M), ACT.Copy,
                                       scale=-1.0).then_inc(s["w_ready"], 1)

                def ln_sq(_):
                    if b is not None:
                        act.wait_ge(s["b_cen"], b + 1)
                        act.activation(sq2[:, :, :], cen2[:, :, :], ACT.Square).then_inc(s["b_sq"], 1)

                def x2t_out(_):
                    if b is not None:
                        act.wait_ge(s["x2t_done"], b + 1)
                        act.activation(x2t[:, :], ps[YB][:, :], ACT.Copy).then_inc(s["x2t_ready"], 1)

                def router(_):
                    if b is not None:
                        act.wait_ge(s["r_in"], b + 1)
                        act.activation(rt[:, :, :], rs[:, :, :], ACT.Exp).then_inc(s["r_ex"], 1)

                steps = {"reload": reload, "sig": gate, "fir": fir, "delta": delta, "square": square, "gelu": hidden, "exp": exp_in,
                         "mix_sq": mix_sq, "moved": moved, "k_silu": beside(k_silu), "q_silu": beside(q_silu),
                         "qk_sq": beside(qk_squares), "tanh": tanh, "y_out": y_out, "w_out": w_out, "ln_sq": ln_sq,
                         "x2t": x2t_out, "router": router}

                def run(items):
                    for what, i in items:
                        if what in steps:
                            steps[what](i)

                def store():
                    if b is not None:
                        act.wait_ge(s["acc_done"], b * E + E)
                        act.dma_start(out_d[:, bass.ds(b * NT, NT), :], x1[:, :, :]).then_inc(s["out_stored"], 16)

                run(START)
                if t is None:
                    run(ALONE)
                    return store()
                for n in range(NC):
                    if t is not None:
                        act.wait_ge(s["u_done"], t * NC + n + 1)
                        if n:
                            act.wait_ge(s["o_done"], t * NC + n)
                        act.activation(u_sb[:, :, :], ps[4][:, 0:2 * DH].rearrange("p (b d) -> p b d", b=2),
                                       ACT.Copy).then_inc(u_ready[n], 1)
                    run(SCAN[2 * n])
                    if t is not None and n < NC - 1:
                        act.wait_ge(s["s_done"], t * (NC - 1) + n + 1)
                        if n:
                            act.wait_ge(s["o_done"], t * NC + n + 1)
                        act.activation(s_sb[:, :, :], ps[3][:, 0:2 * DH].rearrange("p (b d) -> p b d", b=2),
                                       ACT.Copy).then_inc(s_ready[n], 1)
                    run(SCAN[2 * n + 1])
                run(TAIL if u is not None else LAST_TAIL)
                store()

            pipeline(act, body)
            act.wait_ge(s["out_stored"], 16 * NPAIR)

        @block.vector
        def _(dve):
            def flat(a):
                return a.rearrange("p m c -> p (m c)")

            def scaled(dst, src, k):
                for j in range(4):
                    dve.tensor_tensor(dst[:, j, :], src, taps[:, k, j, :], ALU.mult).then_inc(s["w_scaled"], 1)

            norm = chained(dve, "v_vec", 0, 4 + 2 * NPAIR)

            def centre(g):
                part = PARTS[g]
                xt = x_sb[:, part, :]
                dve.wait_ge(s[("x_first_loaded", "x_rest_loaded")[g]], 16)
                norm(dve.tensor_reduce(st[:, 0, part], xt, AX.X, ALU.add))
                dve.scalar_tensor_tensor(xn[:, part, :], st[:, 0, part].unsqueeze(2).to_broadcast([P, part.stop - part.start, D]),
                                         -1.0 / D, xt, ALU.mult, ALU.add).then_inc(s["ln_cen"], 1)

            def variance(g):
                v = st[:, 1, PARTS[g]]
                dve.wait_ge(s["ln_sq"], g + 1)
                norm(dve.tensor_reduce(v, xsq[:, PARTS[g], :], AX.X, ALU.add))
                dve.tensor_scalar(v, v, 1.0 / D, 1e-5, ALU.mult, ALU.add).then_inc(s["ln_ms"], 1)

            def normal(g):
                part = PARTS[g]
                rows = xn[:, part, :]
                dve.wait_ge(s["ln_rs"], g + 1)
                dve.tensor_tensor(rows, rows, st[:, 2, part].unsqueeze(2).to_broadcast([P, part.stop - part.start, D]),
                                  ALU.mult).then_inc(s["xn_ready"], 1)

            centre(0)
            variance(0)
            dve.wait_ge(s["early_loaded"], 32)
            dve.wait_ge(s["late_loaded"], 16)
            normal(0)
            scaled(wkc, wk_sb, 1)
            scaled(wqc, wq_sb, 0)
            dve.tensor_copy(wbe[:, :, :], wb_sb.unsqueeze(2).to_broadcast([P, H, C])).then_inc(s["w_scaled"], 1)
            centre(1)
            scaled(wvc, wv_sb, 2)
            variance(1)

            def project_v(i):
                v, f = vf[i % 2], sf[i % 2]
                dve.wait_ge(s["v_silu"], i + 1)
                for b in range(2):
                    ins = dve.transpose(v_hc[:, 2 * i + b, 2:2 + NC, :].rearrange("p n c -> p (n c)"), v[:, b, 2:2 + L])
                ins.then_inc(s["v_ready"], 1)
                dve.wait_ge(s["short_first"], i + 1)
                norm(dve.scalar_tensor_tensor(f, v[:, :, 1:1 + L], fs_sb[:, 1:2], f, ALU.mult, ALU.add))
                norm(dve.scalar_tensor_tensor(f, v[:, :, 2:2 + L], fs_sb[:, 2:3], f, ALU.mult, ALU.add))
                dve.transpose(short_hc[:, M * i:M * i + M, :].rearrange("p m d -> p (m d)"),
                              f.rearrange("p b l -> p (b l)")).then_inc(s["short_ready"], 1)

            def k_hc(u):
                dve.wait_ge(s["k_silu"], u + 1)
                dve.transpose(flat(qk_hc[:, 1, :, :]), flat(kf[:, :, :])).then_inc(s["qk_ready"], 1)

            def q_hc(u):
                dve.wait_ge(s["q_silu"], u + 1)
                dve.transpose(flat(qk_hc[:, 0, :, :]), flat(qf[:, :, :])).then_inc(s["qk_ready"], 1)

            def norms(u, chain):
                dve.wait_ge(s["qk_squared"], u + 1)
                chain(dve.tensor_reduce(ss[:, :, :], qk_sq[:, :, :, :], AX.X, ALU.add))
                dve.tensor_scalar(ss[:, :, :], ss[:, :, :], 1e-6, None, ALU.add).then_inc(s["ms_ready"], 1)

            def to_hc(u, chain):
                k_hc(u)
                q_hc(u)
                norms(u, chain)

            def to_beta(u, chain):
                dve.wait_ge(s["b_tanh"], u + 1)
                freed(dve, "vb_ready", u)
                chain(dve.transpose(flat(beta[:, :, :]), flat(tb[:, :, :])))
                dve.tensor_scalar(beta[:, :, :], beta[:, :, :], 0.5, 0.5, ALU.mult, ALU.add).then_inc(s["beta_ready"], 1)

            def normalise(u, chain):
                dve.wait_ge(s["rn_ready"], u + 1)
                freed(dve, "moved", u)
                chain(dve.tensor_tensor(kn_next[:, :, :], qk_hc[:, 1, :, :],
                                        rn[:, 1, :].unsqueeze(2).to_broadcast([P, M, DH]), ALU.mult))
                dve.transpose(flat(kq_t[:, 0, :, :]), flat(kn_next[:, :, :]))
                chain(dve.tensor_tensor(qk_hc[:, 0, :, :], qk_hc[:, 0, :, :],
                                        rn[:, 0, :].unsqueeze(2).to_broadcast([P, M, DH]), ALU.mult))
                dve.transpose(flat(kq_t[:, 1, :, :]), flat(qk_hc[:, 0, :, :])).then_inc(s["kq_ready"], 1)
                dve.wait_ge(s["beta_ready"], u + 1)
                freed(dve, "w_done", u)
                dve.tensor_tensor(kb[:, :, :], kn_next[:, :, :], beta[:, :, :], ALU.mult).then_inc(s["kb_ready"], 1)

            def masks(u, chain):
                dve.wait_ge(s["nbm_ready"], u + 1)
                for k in range(2):
                    dve.wait_ge(s["g_done"], u * 2 + k + 1)
                    g = ps[k][:, :].rearrange("p (m a j) -> p m a j", m=8, a=2)
                    ins = dve.tensor_tensor(a_hc[:, 8 * k:8 * k + 8, :], g[:, :, 0, :], nbm[:, 8 * k:8 * k + 8, :],
                                            ALU.mult)
                    if k == 0:
                        chain(ins)
                    else:
                        ins.then_inc(s["a_ready"], 1)
                dve.wait_ge(s["a_ready"], u + 1)
                dve.transpose(flat(a_t[:, :, :]), flat(a_hc[:, :, :])).then_inc(s["at_ready"], 1)
                for k in range(2):
                    g = ps[k][:, :].rearrange("p (m a j) -> p m a j", m=8, a=2)
                    ins = dve.tensor_tensor(attn_next[:, 8 * k:8 * k + 8, :], g[:, :, 1, :],
                                            keep_up[:, :].unsqueeze(1).to_broadcast([P, 8, C]), ALU.mult)
                    if k == 0:
                        chain(ins)
                    else:
                        ins.then_inc(s["attn_ready"], 1)
                chain.end()

            first = chained(dve, "a1_vec", 0, A1_VEC)
            k_hc(0)
            normal(1)
            q_hc(0)
            norms(0, first)
            project_v(0)
            to_beta(0, first)
            normalise(0, first)
            project_v(1)
            project_v(2)
            dve.wait_ge(s["pool_consts"], ALL_CONSTS)
            dve.wait_ge(s["consts_ready"], 1)

            masks(0, first)
            project_v(3)
            norm.end()

            dve.wait_ge(s["temp_act"], 4)
            step = chained(dve, "stats_zero", 0, 7)
            step(dve.tensor_scalar(temp[:, 0:1], logt, 0.0, None, ALU.max))
            step(dve.tensor_tensor(temp[:, 0:1], temp[:, 0:1], temp[:, 3:4], ALU.add))
            step(dve.tensor_scalar(temp[:, 0:1], temp[:, 0:1], 1e-4, None, ALU.add))
            step(dve.reciprocal(temp[:, 1:2], temp[:, 0:1]))
            step(dve.tensor_scalar(floor_hc, floor_hc, 0.05, None, ALU.mult))
            step(dve.tensor_copy(w2e[:, :, :, 0:NP], w2r.rearrange("p (k h j) -> p k h j", k=2, h=H)))
            step(dve.tensor_tensor(wo_sb, wo_sb, on_sb.to_broadcast([P, D]), ALU.mult))
            step.end()

            dve.wait_ge(s["long_ready"], 2)
            ahead = chained(dve, "a1_vec", 1, A1_VEC)
            to_hc(1, ahead)

            def body(u, t, b):
                if u is not None:
                    first = ahead if b is None else chained(dve, "a1_vec", u, A1_VEC)
                if t is not None:
                    chain = chained(dve, "a2_vec", t, A2_VEC)
                if b is not None:
                    chain_b = chained(dve, "b_vec", b, B_VEC)
                chain_m = {last: chained(dve, "mix_vec", pair, MIX_VEC)
                           for last in (0, 1) if (pair := mixed(t, b, last)) is not None}

                def weigh(_):
                    if b is None:
                        return
                    dve.wait_ge(s["r_ex"], b + 1)
                    chain_b(dve.tensor_reduce(st2[:, 3, :], rt[:, :, :], AX.X, ALU.add))
                    chain_b(dve.reciprocal(st2[:, 3, :], st2[:, 3, :]))
                    chain_b(dve.tensor_tensor(rt[:, :, :], rt[:, :, :], st2[:, 3, :].unsqueeze(2).to_broadcast([P, NT, E]),
                                              ALU.mult))
                    for j in range(NT):
                        of = rt[:, j:j + 1, :].to_broadcast([P, E, E])
                        oe = rt[:, j, :].unsqueeze(2).to_broadcast([P, E, E])
                        dve.tensor_tensor(cmp[:, j, :, :], of, oe, ALU.is_ge)
                        ins = dve.tensor_tensor(cmq[:, j, :, :], of, oe, ALU.is_gt)
                    chain_b(ins)
                    fl = "p j e f -> p j (e f)"
                    bc = [P, NT, E * E]
                    chain_b(dve.tensor_tensor(cmp[:, :, :, :].rearrange(fl), cmp[:, :, :, :].rearrange(fl),
                                              before[:, :, :].rearrange("p e f -> p (e f)").unsqueeze(1).to_broadcast(bc),
                                              ALU.mult))
                    chain_b(dve.tensor_tensor(cmq[:, :, :, :].rearrange(fl), cmq[:, :, :, :].rearrange(fl),
                                              after[:, :, :].rearrange("p e f -> p (e f)").unsqueeze(1).to_broadcast(bc),
                                              ALU.mult))
                    chain_b(dve.tensor_tensor(cmp[:], cmp[:], cmq[:], ALU.add))
                    chain_b(dve.tensor_reduce(ru[:, :, :], cmp[:, :, :, :], AX.X, ALU.add))
                    chain_b(dve.scalar_tensor_tensor(rs[:, :, :], ru[:, :, :], 1.5, rt[:, :, :], ALU.is_lt, ALU.mult))
                    chain_b(dve.tensor_reduce(st2[:, 3, :], rs[:, :, :], AX.X, ALU.add))
                    chain_b(dve.tensor_scalar(st2[:, 3, :], st2[:, 3, :], 1e-8, None, ALU.add))
                    chain_b(dve.reciprocal(st2[:, 3, :], st2[:, 3, :]))
                    chain_b(dve.tensor_tensor(rs[:, :, :], rs[:, :, :], st2[:, 3, :].unsqueeze(2).to_broadcast([P, NT, E]),
                                              ALU.mult))
                    chain_b.end()

                def value(i):
                    if b is None:
                        return
                    e, f = i // FC, i % FC
                    dve.wait_ge(s["sg_ready"], b * E * FC + i + 1)
                    dve.wait_ge(s["val_done"], b * E * FC + i + 1)
                    if e >= 2:
                        dve.wait_ge(s["y2_done"], b * E + e - 1)
                    dve.tensor_tensor(fu[:, e % 2, f, :], sg[:, i % 2, :], ps[VALUE[bank_of(u, i)]][:, :],
                                      ALU.mult).then_inc(s["fu_ready"], 1)

                def down(e):
                    if b is None:
                        return
                    dve.wait_ge(s["y2_done"], b * E + e + 1)
                    if e >= 1:
                        dve.wait_ge(s["acc_done"], b * E + e)
                    for j in range(NT):
                        ins = dve.scalar_tensor_tensor(x1[:, j, :], ps[out_bank(t, e)][:, P * j:P * j + P], rs[:, j, e:e + 1],
                                                       x1[:, j, :], ALU.mult, ALU.add)
                    ins.then_inc(s["acc_done"], 1)

                def norm(_):
                    if u is not None:
                        normalise(u, first)

                def masked(_):
                    if u is not None:
                        masks(u, first)

                def path(p, pair):
                    if p == 2:
                        return delta_hc[:, :, :].rearrange("p (b n) d -> p b n d", b=2)
                    if p == 3:
                        return v_hc[:, bass.ds(pair * 2, 2), 2:2 + NC, :]
                    return (short_hc, long_hc)[p][:, bass.ds(pair * M, M), :].rearrange("p (b n) d -> p b n d", b=2)

                def by_batch(a):
                    return a.rearrange("p (b n) d -> p b n d", b=2)

                def centre(p):
                    if t is None:
                        return
                    if p in (1, 3):
                        dve.wait_ge(s["long_ready"], 4 if p == 1 else 3)
                    if p == 2:
                        dve.wait_ge(s["delta_ready"], t + 1)
                    mean = pmean[:, p, :].rearrange("p (b n) -> p b n", b=2)
                    chain(dve.tensor_reduce(mean, path(p, t), AX.X, ALU.add))
                    dve.scalar_tensor_tensor(by_batch(pcen[:, p, :, :]), mean.unsqueeze(3).to_broadcast([P, 2, NC, DH]),
                                             -1.0 / DH, path(p, t), ALU.mult, ALU.add).then_inc(s["cen_ready"], 1)
                    dve.tensor_scalar(stats[:, :, 2 * p], pmean[:, p, :], 1.0 / DH, None, ALU.mult)

                def spread(p):
                    if t is None:
                        return
                    dve.wait_ge(s["psq_ready"], t * NP + PATHS.index(p) + 1)
                    chain(dve.tensor_reduce(pvar[:, p, :], psq[:, p, :, :], AX.X, ALU.add))
                    chain(dve.tensor_scalar(stats[:, :, 2 * p + 1], pvar[:, p, :], 1.0 / DH, None, ALU.mult))

                def stats_out(_):
                    if t is not None:
                        dve.transpose(flat(stats_t[:, :, :]), flat(stats[:, :, :])).then_inc(s["stats_ready"], 1)

                def exp_in(_):
                    if t is None:
                        return
                    dve.wait_ge(s["lg_done"], t + 1)
                    chain(dve.transpose(flat(lg[:, :, :]), ps[4][:, :]))
                    chain(dve.tensor_tensor(lb[:, :, :], lg[:, :, 0:NP], bias_hc.unsqueeze(1).to_broadcast([P, M, NP]),
                                            ALU.add))
                    chain(dve.tensor_reduce(g0[:, :], lb[:, :, :], AX.X, ALU.max))
                    dve.tensor_tensor(lb[:, :, :], lb[:, :, :], g0[:, :].unsqueeze(2).to_broadcast([P, M, NP]),
                                      ALU.subtract).then_inc(s["ex_in"], 1)

                def softmax(_):
                    if t is None:
                        return
                    dve.wait_ge(s["ex_out"], t + 1)
                    for again in range(2):
                        chain(dve.tensor_reduce(g0[:, :], pr[:, :, :], AX.X, ALU.add))
                        chain(dve.reciprocal(g0[:, :], g0[:, :]))
                        chain(dve.tensor_tensor(pr[:, :, :], pr[:, :, :], g0[:, :].unsqueeze(2).to_broadcast([P, M, NP]),
                                                ALU.mult))
                        if not again:
                            chain(dve.tensor_tensor(pr[:, :, :], pr[:, :, :],
                                                    floor_hc.unsqueeze(1).to_broadcast([P, M, NP]), ALU.max))
                    chain.end()

                def mix(part):
                    def step(last):
                        pair = mixed(t, b, last)
                        if pair is None:
                            return
                        for p in ((0, 1), (2, 3), ())[part]:
                            weight = pr[:, :, p:p + 1].rearrange("p (b n) i -> p b n i", b=2)
                            ins = dve.tensor_tensor(by_batch(pcen[:, p, :, :]), path(p, pair),
                                                    weight.to_broadcast([P, 2, NC, DH]), ALU.mult)
                        if part < 2:
                            chain_m[last](ins)
                        else:
                            chain_m[last](dve.tensor_tensor(pcen[:, 0:2, :, :], pcen[:, 0:2, :, :], pcen[:, 2:4, :, :],
                                                              ALU.add))
                            dve.tensor_tensor(oh[:, :, :], pcen[:, 0, :, :], pcen[:, 1, :, :],
                                              ALU.add).then_inc(s["mix_ready"], 1)
                    return step

                def mean_square(last):
                    pair = mixed(t, b, last)
                    if pair is not None:
                        dve.wait_ge(s["osq_ready"], pair + 1)
                        chain_m[last](dve.tensor_reduce(gm[:, :], psq[:, 0, :, :], AX.X, ALU.add))
                        dve.tensor_scalar(gm[:, :], gm[:, :], 1.0 / DH, 1e-5, ALU.mult, ALU.add).then_inc(s["om_ready"], 1)

                def scale(last):
                    pair = mixed(t, b, last)
                    if pair is not None:
                        dve.wait_ge(s["orn_ready"], pair + 1)
                        chain_m[last](dve.tensor_tensor(oh[:, :, :], oh[:, :, :],
                                                          g1[:, :].unsqueeze(2).to_broadcast([P, M, DH]), ALU.mult))
                        dve.transpose(o_t[:, :], flat(oh[:, :, :])).then_inc(s["ot_ready"], 1)
                        chain_m[last].end()

                def output(_):
                    if b is not None:
                        dve.wait_ge(s["wo_done"], b + 1)
                        freed(dve, "out_stored", b * 16)
                        dve.tensor_tensor(x1[:, :, :], ps[YB][:, :].rearrange("p (j d) -> p j d", j=NT),
                                          x_sb[:, bass.ds(b * NT, NT), :], ALU.add).then_inc(s["x1_ready"], 1)

                def t16t(_):
                    if t is not None:
                        dve.wait_ge(s["t16_loaded"], t * 16 + 16)
                        dve.transpose(flat(t16_t[:, :, :]), flat(t16[:, :, :])).then_inc(s["t16t_ready"], 1)

                def v_beta(_):
                    if t is not None:
                        dve.tensor_tensor(vb[:, :, :].rearrange("p (b n) d -> p b (n d)", b=2),
                                          v_hc[:, bass.ds(t * 2, 2), 2:2 + NC, :].rearrange("p b n d -> p b (n d)"),
                                          beta[:, :, :].rearrange("p (b n) d -> p b (n d)", b=2),
                                          ALU.mult).then_inc(s["vb_ready"], 1)

                def t32_add(_):
                    if t is not None:
                        dve.wait_ge(s["t16t_ready"], t + 1)
                        dve.wait_ge(s["t32_done"], t + 1)
                        dve.tensor_tensor(t32_t[:, :, :], ps[2][:, :].rearrange("p (m t) -> p m t", m=M), t16_t[:, :, :],
                                          ALU.add).then_inc(s["t32_ready"], 1)

                def beside(step, *more):
                    return lambda _: step(u, *more) if b is not None and u is not None else None

                def beta_hc(_):
                    if u is not None:
                        to_beta(u, first)

                def ln_cen(_):
                    if b is not None:
                        dve.wait_ge(s["x1_ready"], b + 1)
                        chain_b(dve.tensor_reduce(st2[:, 0, :], x1[:, :, :], AX.X, ALU.add))
                        dve.scalar_tensor_tensor(cen2[:, :, :], st2[:, 0, :].unsqueeze(2).to_broadcast([P, NT, D]), -1.0 / D,
                                                 x1[:, :, :], ALU.mult, ALU.add).then_inc(s["b_cen"], 1)

                def ln_var(_):
                    if b is not None:
                        dve.wait_ge(s["b_sq"], b + 1)
                        chain_b(dve.tensor_reduce(st2[:, 1, :], sq2[:, :, :], AX.X, ALU.add))
                        dve.tensor_scalar(st2[:, 1, :], st2[:, 1, :], 1.0 / D, 1e-5, ALU.mult, ALU.add).then_inc(s["b_ms"], 1)

                def ln_out(_):
                    if b is not None:
                        dve.wait_ge(s["b_rs"], b + 1)
                        dve.tensor_tensor(cen2[:, :, :], cen2[:, :, :], st2[:, 2, :].unsqueeze(2).to_broadcast([P, NT, D]),
                                          ALU.mult).then_inc(s["xn2_ready"], 1)

                def x2_parts(_):
                    if b is not None:
                        dve.wait_ge(s["x2t_ready"], b + 1)
                        dve.tensor_copy(x2_hi[:, :].bitcast(F32R), x2t[:, :]).then_inc(s["x2_split"], 1)
                        dve.wait_ge(s["x2_split"], b * 2 + 1)
                        dve.tensor_tensor(x2_lo[:, :].bitcast(F32R), x2t[:, :], x2_hi[:, :],
                                          ALU.subtract).then_inc(s["x2_split"], 1)

                def router(_):
                    if b is not None:
                        dve.wait_ge(s["r_done"], b + 1)
                        chain_b(dve.tensor_reduce(st2[:, 3, :], ps[YB][:, 0:NT * E].rearrange("p (j e) -> p j e", e=E),
                                                  AX.X, ALU.max))
                        dve.tensor_tensor(rs[:, :, :], ps[YB][:, 0:NT * E].rearrange("p (j e) -> p j e", e=E),
                                          st2[:, 3, :].unsqueeze(2).to_broadcast([P, NT, E]),
                                          ALU.subtract).then_inc(s["r_in"], 1)

                def parts_of(k):
                    if b is None:
                        high, low = ((w11_sb, w11_lo), (w12_sb, w12_lo))[k]
                        dve.wait_ge(s["raw_loaded"], 16 * k + 16)
                        dve.tensor_copy(high[:, :, :].bitcast(F32R), raw).then_inc(s["w_split"], 1)
                        dve.wait_ge(s["w_split"], 2 * k + 1)
                        dve.tensor_tensor(low[:, :, :].bitcast(F32R), raw, high[:, :, :],
                                          ALU.subtract).then_inc(s["w_split"], 1)

                steps = {"split": parts_of, "fuse": value, "add": down, "norm": norm, "mask": masked, "weigh": weigh, "centre": centre,
                         "spread": spread, "stats": stats_out, "exp_in": exp_in, "softmax": softmax, "mix0": mix(0),
                         "mix1": mix(1), "mix2": mix(2), "scale0": mean_square, "scale1": scale, "out": output,
                         "t16t": t16t, "vb": v_beta, "t32_add": t32_add, "k_hc": beside(k_hc), "q_hc": beside(q_hc),
                         "norms": beside(norms, first if u is not None else None), "beta_hc": beta_hc, "ln_cen": ln_cen,
                         "ln_var": ln_var, "ln_out": ln_out, "x2t": x2_parts, "router": router}

                def run(items):
                    for what, i in items:
                        steps.get(what, lambda _: None)(i)

                run(START)
                if t is None:
                    return run(ALONE)
                for items in SCAN:
                    run(items)
                run(TAIL if u is not None else LAST_TAIL)

            pipeline(dve, body)


_OUT = (B, L, D)


def kernel(**inputs):
    import numpy as np
    import concourse.bacc as bacc
    from concourse.bass_utils import run_bass_kernel_spmd

    a = {k.split("_", 2)[2]: np.asarray(v) for k, v in inputs.items()}

    def heads(v):
        return np.repeat(v.reshape(H, -1), C, axis=0)

    w1 = a["gate_w1"].T
    w1s = np.pad(w1[D:].reshape(NP, H, 2, HID).transpose(1, 0, 2, 3).reshape(H, 2 * NP, HID),
                 ((0, 0), (0, C - 2 * NP), (0, 0))).reshape(P, HID)
    early = np.concatenate([a["Wv"].T, a["Wb"].T, a["fir_short_w"].reshape(D, KS)], axis=1)
    late = np.concatenate([a["Wq"].T, a["Wk"].T, a["Wo"].T, w1[:D], w1s, a["gate_b1"].reshape(2, P).T,
                           a["gate_w2"].T.reshape(2, P, H * NP).transpose(1, 0, 2).reshape(P, 2 * H * NP), a["Wg"],
                           heads(a["base_bias"]), heads(a["floor_raw"]), heads(a["log_temp"]),
                           np.tile(a["onorm_w"], H).reshape(P, 1)], axis=1)
    taps = np.concatenate([a[n].T.reshape(-1) for n in ("qconv_w", "kconv_w", "vconv_w")])
    laid = [("x", a["hidden_states"]), ("early", early), ("taps", taps), ("late", late),
            ("flr", a["fir_long_w"].reshape(D, KL)[:, ::-1]), ("w11", a["W11"]), ("w12", a["W12"]), ("w2", a["W2"])]
    nc = bacc.Bacc("TRN2", target_bir_lowering=False, num_devices=1)
    arrays, args = {}, []
    for name, v in laid:
        v = np.ascontiguousarray(v)
        arrays[f"in_{name}"] = v
        args.append(nc.dram_tensor(f"in_{name}", v.shape, mybir.dt.from_np(v.dtype), kind="ExternalInput").ap())
    args.append(nc.dram_tensor("out_y", _OUT, F32, kind="ExternalOutput").ap())
    build(nc, *args)
    r = run_bass_kernel_spmd(nc, [arrays], core_ids=[0])
    return r.results[0]["out_y"]
```
